# Optimizing a Trainium2 kernel written in Bass

```python
import numpy as np
import jax
import jax.numpy as jnp

def _softmax(x, axis=-1):
    return jax.nn.softmax(x, axis=axis)

def _gelu(x):
    return jax.nn.gelu(x, approximate=True)

def _silu(x):
    return jax.nn.silu(x)

def _sigmoid(x):
    return jax.nn.sigmoid(x)

def _layernorm(x, axis=-1, eps=1e-05):
    m = jnp.mean(x, axis=axis, keepdims=True)
    v = jnp.var(x, axis=axis, keepdims=True)
    return (x - m) / jnp.sqrt(v + eps)

def _scatter_add(tgt, idx, src, axis=0):
    return tgt.at[idx].add(src)

def _segment_sum(src, seg, n):
    return jax.ops.segment_sum(src, seg, n)
kernel_name = 'mk_adaln_d1_jaxref_r4_254cea'

def setup_inputs(seed: int=0):
    np.random.seed(seed)
    _w = jnp.asarray

    def _L0_attn_setup():
        import jax, jax.numpy as jnp
        import numpy as np
        D = 256
        H = 16
        HD = D // H
        B = 2
        T = 512

        def _apply_rotary(x, rope):
            x1, x2 = (x[..., ::2], x[..., 1::2])
            sin, cos = (rope[..., ::2], rope[..., 1::2])
            return jnp.concatenate([x1 * cos - x2 * sin, x1 * sin + x2 * cos], axis=-1)
        key = jax.random.key(seed)
        k0, k1, k2 = jax.random.split(key, 3)
        s = 1.0 / np.sqrt(D)
        return {'x': jax.random.normal(k0, (B, T, D), dtype=jnp.float32), 'qkv_w': jax.random.normal(k1, (D, 3 * D), dtype=jnp.float32) * s, 'qkv_b': jnp.zeros((3 * D,), dtype=jnp.float32), 'out_w': jax.random.normal(k2, (D, D), dtype=jnp.float32) * s, 'out_b': jnp.zeros((D,), dtype=jnp.float32)}
    _L0_attn_in = _L0_attn_setup()

    def _L0_ffn_setup():
        import jax, jax.numpy as jnp
        import numpy as np
        B, S, H = (1, 512, 256)
        E = 16
        I = 192
        TOPK = 4
        G = 4
        TOPK_G = 2
        SCALE = 2.5
        N_SHARED = 1

        def _route(x, gate_w, gate_bias):
            n = x.shape[0]
            logits = jnp.einsum('nh,eh->ne', x.astype(jnp.float32), gate_w)
            scores = jax.nn.sigmoid(logits)
            sb = scores + gate_bias
            gs = sb.reshape(n, G, E // G)
            group_scores = jnp.sum(jax.lax.top_k(gs, 2)[0], axis=-1)
            _, gidx = jax.lax.top_k(group_scores, TOPK_G)
            gmask = jnp.sum(jax.nn.one_hot(gidx, G, dtype=sb.dtype), axis=1)
            emask = jnp.repeat(gmask, E // G, axis=-1)
            masked = jnp.where(emask > 0, sb, -jnp.inf)
            _, tidx = jax.lax.top_k(masked, TOPK)
            w = jnp.take_along_axis(scores, tidx, axis=1)
            w = w / (jnp.sum(w, axis=-1, keepdims=True) + 1e-20)
            return (tidx, w * SCALE)
        key = jax.random.key(seed)
        ks = jax.random.split(key, 9)

        def rn(k, shape, scale=0.02):
            return jax.random.normal(k, shape, dtype=jnp.float32) * scale
        return dict(hidden_states=jax.random.normal(ks[0], (B, S, H), dtype=jnp.float32), gate_w=rn(ks[1], (E, H)), gate_bias=jax.random.normal(ks[2], (E,), dtype=jnp.float32) * 0.1, w1=rn(ks[3], (E, I, H)), w2=rn(ks[4], (E, H, I)), w3=rn(ks[5], (E, I, H)), ws1=rn(ks[6], (I * N_SHARED, H)), ws2=rn(ks[7], (H, I * N_SHARED)), ws3=rn(ks[8], (I * N_SHARED, H)))
    _L0_ffn_in = _L0_ffn_setup()
    _L0_c = _w((lambda *s: np.random.randn(*s).astype(np.float32) * 0.05)(4, 256))
    _L0_wmod = _w((lambda *s: np.random.randn(*s).astype(np.float32) * 0.05)(256, 6 * 256) * 256 ** (-0.5))
    _d = {'L0_attn_x': _L0_attn_in['x'], 'L0_attn_qkv_w': _L0_attn_in['qkv_w'], 'L0_attn_qkv_b': _L0_attn_in['qkv_b'], 'L0_attn_out_w': _L0_attn_in['out_w'], 'L0_attn_out_b': _L0_attn_in['out_b'], 'L0_ffn_gate_w': _L0_ffn_in['gate_w'], 'L0_ffn_gate_bias': _L0_ffn_in['gate_bias'], 'L0_ffn_w1': _L0_ffn_in['w1'], 'L0_ffn_w2': _L0_ffn_in['w2'], 'L0_ffn_w3': _L0_ffn_in['w3'], 'L0_ffn_ws1': _L0_ffn_in['ws1'], 'L0_ffn_ws2': _L0_ffn_in['ws2'], 'L0_ffn_ws3': _L0_ffn_in['ws3'], 'L0_c': _L0_c, 'L0_wmod': _L0_wmod}
    _x0 = _d['L0_attn_x']
    _d['L0_attn_x'] = jax.random.normal(jax.random.fold_in(jax.random.key(seed), 1), (4, 2048, 256), dtype=_x0.dtype)
    del _x0
    return _d

def reference(L0_attn_x, L0_attn_qkv_w, L0_attn_qkv_b, L0_attn_out_w, L0_attn_out_b, L0_ffn_gate_w, L0_ffn_gate_bias, L0_ffn_w1, L0_ffn_w2, L0_ffn_w3, L0_ffn_ws1, L0_ffn_ws2, L0_ffn_ws3, L0_c, L0_wmod):

    def _L0_attn_ref(x, qkv_w, qkv_b, out_w, out_b):
        import jax, jax.numpy as jnp
        import numpy as np
        D = 256
        H = 16
        HD = D // H
        B = 2
        T = 512

        def _apply_rotary(x, rope):
            x1, x2 = (x[..., ::2], x[..., 1::2])
            sin, cos = (rope[..., ::2], rope[..., 1::2])
            return jnp.concatenate([x1 * cos - x2 * sin, x1 * sin + x2 * cos], axis=-1)
        Bx, Tx, Dm = x.shape
        qkv = (x @ qkv_w + qkv_b).reshape(Bx, Tx, 3, H, HD).transpose(2, 0, 3, 1, 4)
        q, k, v = (qkv[0], qkv[1], qkv[2])
        inv_freq = 1.0 / 10000.0 ** (jnp.arange(0, HD, 2, dtype=jnp.float32) / HD)
        t = jnp.arange(Tx, dtype=jnp.float32)
        freqs = t[:, None] * inv_freq[None, :]
        rope = jnp.concatenate([jnp.sin(freqs), jnp.cos(freqs)], axis=-1)
        q = _apply_rotary(q, rope)
        k = _apply_rotary(k, rope)
        scale = HD ** (-0.5)
        scores = jnp.einsum('bhqd,bhkd->bhqk', q, k) * scale
        causal_mask = jnp.triu(jnp.ones((Tx, Tx), dtype=bool), 1)
        scores = jnp.where(causal_mask, -jnp.inf, scores)
        attn = jax.nn.softmax(scores, axis=-1)
        out = jnp.einsum('bhqk,bhkd->bhqd', attn, v)
        out = out.transpose(0, 2, 1, 3).reshape(Bx, Tx, Dm)
        return out @ out_w + out_b

    def _L0_ffn_ref(hidden_states, gate_w, gate_bias, w1, w2, w3, ws1, ws2, ws3):
        import jax, jax.numpy as jnp
        import numpy as np
        B, S, H = (1, 512, 256)
        E = 16
        I = 192
        TOPK = 4
        G = 4
        TOPK_G = 2
        SCALE = 2.5
        N_SHARED = 1

        def _route(x, gate_w, gate_bias):
            n = x.shape[0]
            logits = jnp.einsum('nh,eh->ne', x.astype(jnp.float32), gate_w)
            scores = jax.nn.sigmoid(logits)
            sb = scores + gate_bias
            gs = sb.reshape(n, G, E // G)
            group_scores = jnp.sum(jax.lax.top_k(gs, 2)[0], axis=-1)
            _, gidx = jax.lax.top_k(group_scores, TOPK_G)
            gmask = jnp.sum(jax.nn.one_hot(gidx, G, dtype=sb.dtype), axis=1)
            emask = jnp.repeat(gmask, E // G, axis=-1)
            masked = jnp.where(emask > 0, sb, -jnp.inf)
            _, tidx = jax.lax.top_k(masked, TOPK)
            w = jnp.take_along_axis(scores, tidx, axis=1)
            w = w / (jnp.sum(w, axis=-1, keepdims=True) + 1e-20)
            return (tidx, w * SCALE)
        b, s, h = hidden_states.shape
        x = hidden_states.reshape(-1, h)
        tidx, tw = _route(x, gate_w, gate_bias)
        n = x.shape[0]
        combine = jnp.zeros((n, E), x.dtype).at[jnp.arange(n)[:, None], tidx].add(tw)
        g = jnp.einsum('nh,eih->nei', x, w1)
        u = jnp.einsum('nh,eih->nei', x, w3)
        hact = jax.nn.silu(g) * u * combine[:, :, None]
        y = jnp.einsum('nei,ehi->nh', hact, w2)
        shared = jnp.einsum('ni,hi->nh', jax.nn.silu(x @ ws1.T) * (x @ ws3.T), ws2)
        return (y + shared).reshape(b, s, h)
    x = L0_attn_x
    mod = (_silu(L0_c) @ L0_wmod).reshape(L0_c.shape[0], 6, 1, -1)
    sa, ca, ga, sb, cb, gb = (mod[:, 0], mod[:, 1], mod[:, 2], mod[:, 3], mod[:, 4], mod[:, 5])
    ga = (2 * (ga >= 0) - 1) * jnp.maximum(jnp.abs(ga), 0.25)
    gb = (2 * (gb >= 0) - 1) * jnp.maximum(jnp.abs(gb), 0.25)
    h = _layernorm(x, axis=-1) * (1 + ca) + sa
    x = x + ga * _L0_attn_ref(h, L0_attn_qkv_w, L0_attn_qkv_b, L0_attn_out_w, L0_attn_out_b)
    h = _layernorm(x, axis=-1) * (1 + cb) + sb
    x = x + gb * _L0_ffn_ref(h, L0_ffn_gate_w, L0_ffn_gate_bias, L0_ffn_w1, L0_ffn_w2, L0_ffn_w3, L0_ffn_ws1, L0_ffn_ws2, L0_ffn_ws3)
    return x

_drawn_inputs = setup_inputs


def setup_inputs(seed=0):
    import zlib

    import numpy as np

    out = dict(_drawn_inputs(seed))
    spreads = {'L0_attn_qkv_b': (0.0, 0.306), 'L0_attn_out_b': (0.0, 0.34)}
    factors = {'L0_ffn_gate_w': 8.0,
     'L0_ffn_gate_bias': 8.0,
     'L0_ffn_w1': 8.0,
     'L0_ffn_w2': 8.0,
     'L0_ffn_w3': 8.0,
     'L0_ffn_ws1': 8.0,
     'L0_ffn_ws2': 8.0,
     'L0_ffn_ws3': 8.0}
    for name, (base, spread) in spreads.items():
        noise = np.random.default_rng([zlib.crc32(name.encode()), seed]).standard_normal(out[name].shape)
        drawn = base * np.exp(spread * noise) if base else spread * noise
        out[name] = jnp.asarray(drawn.astype(out[name].dtype))
    for name, factor in factors.items():
        out[name] = (out[name] * factor).astype(out[name].dtype)
    return out
```

```python
from contextlib import ExitStack

import numpy as np

import concourse.bass as bass
from concourse import mybir

F32 = mybir.dt.float32
BF16 = mybir.dt.bfloat16
ALU = mybir.AluOpType
ACT = mybir.ActivationFunctionType
AX = mybir.AxisListType

B, T, D, H, HD = 4, 2048, 256, 16, 16
N = B * T
NT = N // 128
E, I, G = 16, 192, 4
NE = E + 1
BIG = 1e30
EPS = 1e-5


class Queues:

    ENGINES = ("sync", "tensor", "vector", "scalar", "gpsimd")

    def __init__(self, nc, ctx):
        self.nc, self.ctx = nc, ctx
        self.q = {e: [] for e in self.ENGINES}
        self.sem, self.count = {}, {}

    def add(self, engine, fn, after=(), mark=None, dma=False):
        if mark is not None:
            if mark not in self.sem:
                self.sem[mark] = self.ctx.enter_context(self.nc.semaphore(mark))
                self.count[mark] = 0
            self.count[mark] += 16 if dma else 1
        flat = [x for t in after if t is not None for x in ([t] if isinstance(t[0], str) else t)]
        self.q[engine].append((fn, tuple(flat), mark, 16 if dma else 1))
        return None if mark is None else (mark, self.count[mark])

    def everything(self):
        return list(self.count.items())

    def pause(self, engine, tokens):
        self.q[engine].append((None, tuple(tokens), None, 0))

    def play(self, engine, eng):
        seen = {}
        for fn, after, mark, inc in self.q[engine]:
            for name, value in after:
                if seen.get(name, 0) < value:
                    eng.wait_ge(self.sem[name], value)
                    seen[name] = value
            if fn is None:
                continue
            ins = fn(eng)
            if mark is not None:
                ins.then_inc(self.sem[mark], inc)


class Arena:

    def __init__(self, nc, start):
        self.nc, self.at, self.n = nc, start, 0

    def __call__(self, name, shape, dt):
        size = int(np.prod(shape[1:])) * (2 if dt == BF16 else 4)
        size = (size + 31) // 32 * 32
        t = self.nc.alloc_sbuf_tensor_at(name, shape, dt, offset=self.at)
        self.at += size
        return t


def program(nc, x, wqk, wv, bqk, bv, wo, ob, gw, gbias, w13, w2, cT, wmod, ropec, ropes, consts, out):
    parts_d = nc.dram_tensor("qk_parts", [B, H, 2, 3, HD, T], BF16, kind="Internal").ap()
    v_d = nc.dram_tensor("v_rows", [B, 128, T // 128, H * 17], F32, kind="Internal").ap()
    x1_d = nc.dram_tensor("x1_rows", [N, D], F32, kind="Internal").ap()

    with ExitStack() as ctx:
        Q = Queues(nc, ctx)
        PB = ctx.enter_context(nc.psum_tensor("PB", [128, 8, 512], F32))
        probe = nc.sbuf_base
        A = Arena(nc, (int(probe) + 1023) // 1024 * 1024)

        ident = A("ident", [128, 128], F32)
        sel = A("sel", [128, 128], F32)
        identb = A("identb", [128, 128], BF16)
        m1 = A("m1", [128, 128], BF16)
        m2 = A("m2", [128, 128], BF16)
        mT = A("mT", [128, 8, 4], F32)
        GA = A("GA", [128, 4, 256], F32)
        GB = A("GB", [128, 4, 256], F32)
        obB = A("obB", [128, 256], F32)
        wo_s = A("wo_s", [128, 4, 256], F32)
        mhalf = A("mhalf", [128, 4], F32)
        phase_start = A.at

        wm_s = A("wm_s", [128, 2, 1536], F32)
        cT_s = A("cT_s", [128, 2, 4], F32)
        ce = A("ce", [128, 2, 4], F32)
        cd = A("cd", [128, 2, 4], F32)
        cr = A("cr", [128, 2, 4], F32)
        sc = A("sc", [128, 2, 4], F32)
        scb = A("scb", [128, 2, 4, 128], F32)
        cons = A("cons", [128, 4, 128], F32)
        gneg = A("gneg", [128, 4, 256], F32)
        gsg = A("gsg", [128, 4, 256], F32)
        wqk_s = A("wqk_s", [128, 2, 512], F32)
        wv_s = A("wv_s", [128, 2, 256], F32)
        bqk_s = A("bqk_s", [128, 4], F32)
        bvB = A("bvB", [128, 2, 256], F32)
        rC = A("rC", [128, T], F32)
        rS = A("rS", [128, T], F32)
        xt = A("xt", [128, 2, 4, 256], F32)
        st6 = A("st6", [128, 2, 4, 6], F32)
        mv = A("mv", [128, 2, 4, 2], F32)
        ve = A("ve", [128, 2, 4], F32)
        rstd = A("rstd", [128, 2, 4], F32)
        xn = A("xn", [128, 2, 4, 256], F32)
        hT = A("hT", [128, 2, 2, 512], F32)
        ta = A("ta", [128, 2, 512], F32)
        tb = A("tb", [128, 2, 512], F32)
        r = A("r", [128, 2, 4, 512], F32)
        pe_ = A("pe_", [128, 4, 512], F32)
        pt = A("pt", [128, 2, 3, 4, 512], BF16)
        vst = A("vst", [128, 2, 4, 16, 17], F32)

        def load(dst, src, mark):
            return Q.add("sync", lambda e: e.dma_start(dst, src), mark=mark, dma=True)

        load(cT_s[:, :, :], cT, "l_mod")
        load(cons[:, :, :], consts, "l_mod")
        t_mod = load(wm_s[:, :, :], wmod.rearrange("(k p) n -> p k n", p=128), "l_mod")
        xch = x.rearrange("(c t p) d -> c p t d", t=4, p=128)

        x_free = [None, None]

        def load_x(c):
            return Q.add("sync", lambda e: e.dma_start(xt[:, c % 2], xch[c]), after=[x_free[c % 2]],
                         mark=f"l_x{c % 2}", dma=True)

        tx = {0: load_x(0), 1: load_x(1)}
        load(wqk_s[:, :, :], wqk.rearrange("(k p) n -> p k n", p=128), "l_w")
        load(wv_s[:, :, :], wv.rearrange("(k p) n -> p k n", p=128), "l_w")
        load(bqk_s[:, :], bqk, "l_w")
        load(bvB[:, 0, :], bv.partition_broadcast(128), "l_w")
        load(bvB[:, 1, :], bv.partition_broadcast(128), "l_w")
        load(obB[:, :], ob.partition_broadcast(128), "l_w")
        load(wo_s[:, :, :], wo, "l_w")
        load(rC[:, :], ropec, "l_w")
        t_w = load(rS[:, :], ropes, "l_w")

        t = Q.add("scalar", lambda e: e.activation(ce[:, :, :], cT_s[:, :, :], ACT.Exp, scale=-1.0),
                  after=[t_mod], mark="c_exp")
        t = Q.add("vector", lambda e: e.tensor_scalar(cd[:, :, :], ce[:, :, :], 1.0, None, ALU.add),
                  after=[t, t_mod], mark="c_v")
        t = Q.add("vector", lambda e: e.reciprocal(cr[:, :, :], cd[:, :, :]), after=[t], mark="c_v")
        t = Q.add("vector", lambda e: e.tensor_tensor(sc[:, :, :], cT_s[:, :, :], cr[:, :, :], ALU.mult),
                  after=[t], mark="c_v")
        t_sc = t
        t_scb = Q.add("vector", lambda e: e.tensor_copy(scb[:, :, :, :], sc[:, :, :].unsqueeze(3).broadcast_to([128, 2, 4, 128])),
                      after=[t], mark="c_v")
        Q.add("vector", lambda e: e.tensor_copy(ident[:, :], cons[:, 0, :]), mark="c_k")
        Q.add("vector", lambda e: e.tensor_copy(sel[:, :], cons[:, 1, :]), mark="c_k")
        Q.add("vector", lambda e: e.tensor_copy(identb[:, :], cons[:, 0, :]), mark="c_k")
        Q.add("vector", lambda e: e.tensor_copy(m1[:, :], cons[:, 2, :]), mark="c_k")
        Q.add("vector", lambda e: e.tensor_copy(m2[:, :], cons[:, 3, :]), mark="c_k")
        t_half = Q.add("vector", lambda e: e.memset(mhalf[:, :], -0.5), mark="c_k")
        t_k = t_half
        Q.add("vector", lambda e: e.memset(vst[:, :, :, :, 16:17], 1.0), mark="c_k")

        for n, (kind, f) in enumerate([(k, f) for k in (0, 1, 3, 4) for f in (0, 1)]):
            for k in (0, 1):
                col = kind * 256 + f * 128
                t = Q.add("tensor", lambda e, n=n, k=k, col=col: e.matmul(
                    PB[:, 7, 4 * n:4 * n + 4], wm_s[:, k, col:col + 128], sc[:, k, :], start=k == 0, stop=k == 1),
                    after=[t_mod, t_sc], mark="m_mod")
        t_m = t
        t = Q.add("vector", lambda e: e.tensor_copy(mT[:, :, :], PB[:, 7, 0:32].rearrange("p (n b) -> p n b", b=4)),
                  after=[t_m], mark="c_m")
        for n in (2, 3, 6, 7):
            t = Q.add("vector", lambda e, n=n: e.tensor_scalar(mT[:, n, :], mT[:, n, :], 1.0, None, ALU.add),
                      after=[t], mark="c_m")
        t_mT = t
        for n, (kind, dst) in enumerate(((2, GA), (5, GB))):
            for b in range(4):
                bank = 3 + b if n == 0 else 3 + b
                for k in (0, 1):
                    t = Q.add("tensor", lambda e, n=n, k=k, b=b, kind=kind: e.matmul(
                        PB[:, 3 + b // 2 + 2 * n, 256 * (b % 2):256 * (b % 2) + 256], scb[:, k, b, :],
                        wm_s[:, k, kind * 256:kind * 256 + 256], start=k == 0, stop=k == 1),
                        after=[t_scb, t_mT], mark="m_gate")
            src = PB[:, 3 + 2 * n:5 + 2 * n, :].rearrange("p a (b d) -> p (a b) d", d=256)
            t = Q.add("vector", lambda e, dst=dst, src=src: e.tensor_copy(dst[:, :, :], src), after=[t], mark="c_g")
            t = Q.add("vector", lambda e, dst=dst: e.tensor_scalar(gneg[:, :, :], dst[:, :, :], -1.0, None, ALU.mult),
                      after=[t], mark="c_g")
            t = Q.add("vector", lambda e, dst=dst: e.tensor_scalar(gsg[:, :, :], dst[:, :, :], 0.0, 2.0, ALU.is_ge, ALU.mult),
                      after=[t], mark="c_g")
            t = Q.add("vector", lambda e, dst=dst: e.tensor_tensor(gneg[:, :, :], dst[:, :, :], gneg[:, :, :], ALU.max),
                      after=[t], mark="c_g")
            t = Q.add("vector", lambda e: e.tensor_scalar(gneg[:, :, :], gneg[:, :, :], 0.25, None, ALU.max),
                      after=[t], mark="c_g")
            t = Q.add("vector", lambda e, dst=dst: e.scalar_tensor_tensor(
                out=dst[:, :, :], in0=gsg[:, :, :], scalar=-1.0, in1=gneg[:, :, :], op0=ALU.add, op1=ALU.mult),
                after=[t], mark="c_g")
            t_gate = t

        tp_free = [None, None]
        qk_free = [None] * 4
        v_free = [None] * 2
        hT_free = [None, None]
        r_free = [None, None]
        pe_free = None
        pt_free = [None, None]
        vst_free = [None, None]
        xn_free = [None, None]
        ro = [None, None]
        for c in range(16):
            b, s, tok = c // 4, c % 2, (c % 4) * 512
            for i in range(4):
                t = Q.add("vector", lambda e, i=i, s=s: e.bn_stats(st6[:, s, i, :], xt[:, s, i, :]), after=[tx[c]], mark="ln")
            for i in range(4):
                t = Q.add("vector", lambda e, i=i, s=s: e.bn_aggr(mv[:, s, i, :], st6[:, s, i, :]), after=[t], mark="ln")
            t = Q.add("vector", lambda e, s=s: e.tensor_scalar(ve[:, s, :], mv[:, s, :, 1], EPS, None, ALU.add), after=[t], mark="ln")
            t = Q.add("gpsimd", lambda e, s=s: e.tensor_tensor(rstd[:, s, :], ve[:, s, :], mhalf[:, :], ALU.pow),
                      after=[t, t_half], mark="rs")
            for i in range(4):
                t = Q.add("vector", lambda e, i=i, s=s: e.tensor_scalar(
                    xn[:, s, i, :], xt[:, s, i, :], mv[:, s, i, 0:1], rstd[:, s, i:i + 1], ALU.subtract, ALU.mult),
                    after=[t, xn_free[s]], mark="xn")
            x_free[s] = t
            if c + 2 < 16:
                tx[c + 2] = load_x(c + 2)
            for f in (0, 1):
                for i in range(4):
                    tt = Q.add("tensor", lambda e, i=i, f=f, s=s: e.transpose(
                        PB[:, f, 128 * i:128 * i + 128], xn[:, s, i, 128 * f:128 * f + 128], ident[:, :]),
                        after=[t, t_k, tp_free[f]], mark="tp")
                th = Q.add("scalar", lambda e, f=f, s=s, b=b: e.activation(
                    hT[:, s, f, :], PB[:, f, :], ACT.Identity, bias=mT[:, f, b:b + 1], scale=mT[:, 2 + f, b:b + 1]),
                    after=[tt, t_mT, hT_free[s]], mark="hT")
                tp_free[f] = th
            xn_free[s] = tt
            tq = []
            for m in range(4):
                for f in (0, 1):
                    t = Q.add("tensor", lambda e, m=m, f=f, s=s: e.matmul(
                        PB[:, 2 + m, :], wqk_s[:, f, 128 * m:128 * m + 128], hT[:, s, f, :], start=f == 0, stop=f == 1),
                        after=[th, t_w, qk_free[m], t_gate], mark="qk")
                tq.append(t)
            for m in range(2):
                for i in (2 * m, 2 * m + 1):
                    for f in (0, 1):
                        t = Q.add("tensor", lambda e, m=m, i=i, f=f, s=s: e.matmul(
                            PB[:, 6 + m, 256 * (i % 2):256 * (i % 2) + 256], hT[:, s, f, 128 * i:128 * i + 128],
                            wv_s[:, f, :], start=f == 0, stop=f == 1), after=[th, v_free[m]], mark="v")
                v_free[m] = Q.add("vector", lambda e, m=m, s=s: e.tensor_tensor(
                    vst[:, s, 2 * m:2 * m + 2, :, 0:16],
                    PB[:, 6 + m, :].rearrange("p (i h d) -> p i h d", i=2, d=16),
                    bvB[:, :, :].rearrange("p i (h d) -> p i h d", d=16), ALU.add),
                    after=[t, vst_free[s], t_w], mark="vb")
            hT_free[s] = t
            vst_free[s] = Q.add("sync", lambda e, s=s, b=b, c=c: e.dma_start(
                v_d[b, :, 4 * (c % 4):4 * (c % 4) + 4, :], vst[:, s].rearrange("p i h d -> p i (h d)")),
                after=[v_free[1]], mark=f"w_v{s}", dma=True)
            for z in (0, 1):
                lo, hi = 2 + 2 * z, 3 + 2 * z
                C, S = rC[:, tok:tok + 512], rS[:, tok:tok + 512]

                def rot(dst, bank, tab, z=z, s=s):
                    return lambda e: e.scalar_tensor_tensor(out=dst, in0=PB[:, bank, :], scalar=bqk_s[:, bank - 2:bank - 1],
                                                            in1=tab, op0=ALU.add, op1=ALU.mult)
                for half, (tl, th_, op) in enumerate(((C, S, ALU.subtract), (S, C, ALU.add))):
                    Q.add("vector", rot(ta[:, half], lo, tl), after=[tq[2 * z], ro[half]], mark="rot")
                    t = Q.add("vector", rot(tb[:, half], hi, th_), after=[tq[2 * z + 1]], mark="rot")
                    t = Q.add("vector", lambda e, half=half, z=z, s=s, op=op: e.tensor_tensor(
                        r[:, s, 2 * z + half, :], ta[:, half], tb[:, half], op), after=[t, r_free[s]], mark="rot")
                    ro[half] = t
                qk_free[2 * z] = qk_free[2 * z + 1] = t
            t1 = Q.add("scalar", lambda e, s=s: e.activation(pt[:, s, 0], r[:, s], ACT.Copy), after=[t, pt_free[s]], mark="p_hi")
            t2 = Q.add("gpsimd", lambda e, s=s: e.tensor_tensor(pe_[:, :, :], r[:, s], pt[:, s, 0], ALU.subtract),
                       after=[t1, pe_free], mark="p_rest")
            r_free[s] = t2
            t3 = Q.add("scalar", lambda e, s=s: e.activation(pt[:, s, 1], pe_[:, :, :], ACT.Copy), after=[t2], mark="p_mid")
            t4 = Q.add("gpsimd", lambda e, s=s: e.tensor_tensor(pt[:, s, 2], pe_[:, :, :], pt[:, s, 1], ALU.subtract),
                       after=[t3], mark="p_lo")
            pe_free = t4
            for z in (0, 1):
                for k in range(3):
                    for half in (0, 1):
                        dst = parts_d[b, :, z, k, 8 * half:8 * half + 8, tok:tok + 512]
                        pt_free[s] = Q.add("sync", lambda e, s=s, k=k, z=z, half=half, dst=dst: e.dma_start(
                            dst, pt[:, s, k, 2 * z + half, :]), after=[t4], mark=f"w_p{s}", dma=True)

        done_p = Q.everything()

        A.at = phase_start
        V = A("V", [128, 2, 16, 272], F32)
        QO = A("QO", [98, 3, 4, T], BF16)
        KO = A("KO", [98, 3, 4, T], BF16)
        NP = 5
        P = A("P", [128, NP, 2, 512], F32)
        ON = A("ON", [128, 4, T], F32)
        osb = A("osb", [128, 512], F32)
        rden = A("rden", [128, 512], F32)
        mx = A("mx", [128, 4, 16, 4], F32)
        nm = A("nm", [128, 4, 16], F32)
        nh = A("nh", [16, 2, 2, 128], BF16)
        xin = A("xin", [128, 2, 256], F32)
        xo = A("xo", [128, 256], F32)

        for e in Q.ENGINES:
            Q.pause(e, done_p)
        Q.add("vector", lambda e: e.memset(mx[:, :, :, :], -3.0e38), mark="a_mx")
        t_ones = Q.add("vector", lambda e: e.memset(KO[96:98, :, :, :], 1.0), mark="a_ones")
        t_o0 = Q.add("vector", lambda e: e.memset(PB[:, 6:8, :], 0.0), mark="a_o0")
        Q.pause("vector", [("a_mx", 1), t_ones, t_o0])

        def load_v(b, after):
            return Q.add("sync", lambda e: e.dma_start(V[:, b % 2], v_d[b]), after=after, mark=f"l_v{b % 2}", dma=True)

        def load_g(g, after):
            b, h0, s = g // 4, 4 * (g % 4), g % 3
            t = None
            for dst, z, plan in ((QO, 0, ((0, 0, 3), (48, 0, 2), (80, 0, 1))),
                                 (KO, 1, ((0, 0, 1), (16, 0, 1), (32, 0, 1), (48, 1, 1), (64, 1, 1), (80, 2, 1)))):
                for row, k, n in plan:
                    src = parts_d[b, h0:h0 + 4, z, k:k + n].rearrange("h k d t -> (k d) h t")
                    t = Q.add("sync", lambda e, dst=dst, row=row, n=n, s=s, src=src: e.dma_start(
                        dst[row:row + 16 * n, s], src), after=after, mark=f"l_g{s}", dma=True)
            return t

        units = [0]
        unit_read = []

        def unit_bank():
            u = units[0]
            units[0] += 1
            return 4 + u % 2, unit_read[u - 2] if u >= 2 else None

        nm_dma = {}
        loaded = {}

        def max_units(g):
            s = g % 3
            for j in range(4):
                for t in range(16):
                    n_all = 128 * (t + 1)
                    for kc in range((n_all + 511) // 512):
                        def emit(j=j, t=t, kc=kc, n=min(512, n_all - 512 * kc), last=512 * kc + 512 >= n_all):
                            bank, free = unit_bank()
                            tk = Q.add("tensor", lambda e: e.matmul(
                                PB[:, bank, 0:n], QO[0:96, s, j, 128 * t:128 * t + 128],
                                KO[0:96, s, j, 512 * kc:512 * kc + n], start=True, stop=True),
                                after=[loaded[g], free], mark="s")
                            if last:
                                tk = Q.add("tensor", lambda e: e.matmul(
                                    PB[:, bank, n - 128:n], identb[:, :], m1[:, :], start=False, stop=True,
                                    skip_group_check=True), mark="s")
                            unit_read.append(Q.add("vector", lambda e: e.tensor_reduce(
                                mx[:, j, t, kc:kc + 1], PB[:, bank, 0:n], AX.X, ALU.max), after=[tk], mark="mx"))
                        yield emit

                def fin(j=j):
                    tk = Q.add("vector", lambda e: e.tensor_reduce(nm[:, j, :], mx[:, j], AX.X, ALU.max, negate=True),
                               after=[unit_read[-1]], mark="nm")
                    bank, free = unit_bank()
                    tk = Q.add("tensor", lambda e: e.transpose(PB[0:16, bank, 0:128], nm[:, j, :], ident[:, :]),
                               after=[tk, free], mark="s")
                    tk = Q.add("vector", lambda e: e.tensor_copy(nh[:, j % 2, 0, :], PB[0:16, bank, 0:128]),
                               after=[tk, nm_dma.get((g, j - 2) if j > 1 else (g - 1, j + 2))], mark="nh")
                    tk = Q.add("vector", lambda e: e.tensor_tensor(nh[:, j % 2, 1, :], PB[0:16, bank, 0:128], nh[:, j % 2, 0, :],
                                                                   ALU.subtract), after=[tk], mark="mx")
                    unit_read.append(tk)
                    for k in (0, 1):
                        nm_dma[g, j] = Q.add("gpsimd", lambda e, k=k: e.dma_start(
                            QO[96 + k:97 + k, s, j, :].rearrange("o (t q) -> o t q", q=128),
                            nh[:, j % 2, k, :]), after=[tk, loaded[g]], mark=f"w_nm{j}", dma=True)
                yield fin

        st_read = [None, None]
        p_read = [None] * NP
        np_ = [0]
        o_free = [t_o0, t_o0]
        osb_free = [None, None]
        rd_free = [None, None]
        nchunk = [0]
        on_tok = {}
        proj_tok = {}
        x1_free = [None, None]
        xin_free = [None, None]
        xo_free = [None, None]
        xg_free = [None, None]
        ngood = [0]
        store_x1 = []

        def proj_units(b):
            for t in range(16):
                def emit(t=t):
                    k = ngood[0] % 2
                    ngood[0] += 1
                    row = b * T + t * 128
                    tl = Q.add("sync", lambda e: e.dma_start(xin[:, k], x[row:row + 128, :]), after=[xin_free[k]],
                               mark=f"l_xi{k}", dma=True)
                    bank, free = unit_bank()
                    for gi in range(4):
                        tk = Q.add("tensor", lambda e, gi=gi: e.matmul(
                            PB[:, bank, 0:256], ON[:, gi, 128 * t:128 * t + 128], wo_s[:, gi, :], start=gi == 0, stop=gi == 3),
                            after=[free, on_tok[b, 3, t // 4]], mark="s")
                    proj_tok[b, t] = tk
                    ta_ = Q.add("vector", lambda e: e.tensor_tensor(xo[:, :], PB[:, bank, 0:256], obB[:, :], ALU.add),
                                after=[tk, xo_free[0]], mark="mx")
                    unit_read.append(ta_)
                    tb_ = Q.add("gpsimd", lambda e: e.tensor_tensor(xo[:, :], xo[:, :], GA[:, b], ALU.mult),
                                after=[ta_], mark="xg")
                    tc_ = Q.add("gpsimd", lambda e: e.tensor_tensor(xin[:, k], xo[:, :], xin[:, k], ALU.add),
                                after=[tb_, tl], mark="x1")
                    xo_free[0] = tc_
                    xin_free[k] = Q.add("sync", lambda e: e.dma_start(x1_d[row:row + 128, :], xin[:, k]), after=[tc_],
                                       mark=f"w_x1{k}", dma=True)
                yield emit

        t_v = {0: load_v(0, []), 1: None}
        for g in range(3):
            loaded[g] = load_g(g, [])
        t_v[1] = load_v(1, [])
        for emit in max_units(0):
            emit()
        proj = []
        done_g = {}
        def group(g):
            b, s, gi = g // 4, g % 3, g % 4
            if gi == 0 and 1 <= b < 3:
                t_v[b + 1] = load_v(b + 1, [done_g[g - 1]])
            mu = list(max_units(g + 1)) if g < 15 else []
            steps = [(c, kt) for c in range(4) for kt in range(4 * c + 4)]
            pend = []
            late = []

            def st(p, c, kt):
                q0 = max(c * 512, kt * 128)
                n = (c + 1) * 512 - q0
                diag = kt >= 4 * c
                for jj in (0, 1):
                    j = 2 * p + jj
                    tk = Q.add("tensor", lambda e, j=j, q0=q0, n=n: e.matmul(
                        PB[:, j, 0:n], KO[0:98, s, j, 128 * kt:128 * kt + 128], QO[0:98, s, j, q0:q0 + n],
                        start=True, stop=True), after=[loaded[g], nm_dma[g, j], t_ones, st_read[p]], mark="st")
                    if diag:
                        tk = Q.add("tensor", lambda e, j=j: e.matmul(
                            PB[:, j, 0:128], identb[:, :], m2[:, :], start=False, stop=True, skip_group_check=True), mark="st")
                pb = np_[0] % NP
                np_[0] += 1
                st_read[p] = Q.add("scalar", lambda e: e.activation(
                    P[:, pb, :, 0:n], PB[:, 2 * p:2 * p + 2, 0:n], ACT.Exp, scale=0.25),
                    after=[tk, p_read[pb]], mark="exp")
                return pb, st_read[p], q0 - c * 512, n

            def pv(c, kt, pair):
                ob_ = nchunk[0] % 2
                bank = 6 + ob_
                for j in range(4):
                    pb, te, o0, n = pair[j // 2]
                    h = 4 * gi + j
                    tk = Q.add("tensor", lambda e, j=j, pb=pb, o0=o0, n=n, h=h: e.matmul(
                        PB[32 * j:32 * j + 17, bank, o0:512], V[:, b % 2, kt, 17 * h:17 * h + 17], P[:, pb, j % 2, 0:n],
                        start=kt == 0, stop=True, skip_group_check=True),
                        after=[pair[0][1], pair[1][1], o_free[ob_] if kt == 0 else None, t_v[b]], mark="pv")
                for pb, *_ in pair:
                    p_read[pb] = tk
                if kt == 4 * c + 3:
                    nchunk[0] += 1
                    toc = Q.add("scalar", lambda e: e.activation(osb[:, :], PB[:, bank, :], ACT.Copy),
                                after=[tk, osb_free[0]], mark="oc")

                    def norm():
                        td = Q.add("tensor", lambda e: e.matmul(PB[:, bank, :], sel[:, :], osb[:, :], start=True, stop=True,
                                                                skip_group_check=True), after=[toc], mark="den")
                        tr = Q.add("vector", lambda e: e.reciprocal(rden[:, :], PB[:, bank, :]),
                                   after=[td, rd_free[0]], mark="rd")
                        o_free[ob_] = tr
                        need = [proj_tok[b - 1, 4 * c + i] for i in range(4)] if b > 0 else []
                        ton = Q.add("gpsimd", lambda e: e.tensor_tensor(
                            ON[:, gi, 512 * c:512 * c + 512], osb[:, :], rden[:, :], ALU.mult), after=[tr, *need], mark="on")
                        osb_free[0] = rd_free[0] = ton
                        on_tok[b, gi, c] = ton
                    late.append([3, norm])
                return tk

            def tick():
                for x_ in list(late):
                    x_[0] -= 1
                    if x_[0] == 0:
                        late.remove(x_)
                        x_[1]()

            done = 0
            for i, (c, kt) in enumerate(steps):
                want = min(len(mu), -(-len(mu) * (i + 1) // 37))
                p0 = st(0, c, kt)
                half = (want - done) // 2
                for _ in range(half):
                    mu[done]()
                    done += 1
                if len(pend) == 2:
                    pv(*pend.pop(0))
                p1 = st(1, c, kt)
                while done < want:
                    mu[done]()
                    done += 1
                pend.append((c, kt, (p0, p1)))
                if i >= 4:
                    for _ in range(2):
                        if proj:
                            proj.pop(0)()
                tick()
            for x_ in pend:
                tk = pv(*x_)
                tick()
            while late:
                tick()
            done_g[g] = tk
            if g + 3 < 16:
                loaded[g + 3] = load_g(g + 3, [done_g[g]])
            if gi == 3:
                assert not proj
                proj.extend(proj_units(b))
        for g in range(16):
            group(g)
        for emit in proj:
            emit()
        done_a = Q.everything()

        A.at = phase_start
        W13 = A("W13", [128, 2, NE, 2 * I], F32)
        W2 = A("W2", [128, NE, 2, 256], F32)
        h2T = A("h2T", [128, NT, 2, 128], F32)
        L = A("L", [128, NT, 16], F32)
        sg = A("sg", [128, NT, 16], F32)
        sb_ = A("sb_", [128, NT, 16], F32)
        rk = A("rk", [128, NT, 16], F32)
        cm = A("cm", [128, NT, 16], F32)
        gs = A("gs", [128, NT, 4], F32)
        gt = A("gt", [128, NT, 4], F32)
        gr = A("gr", [128, NT, 4], F32)
        wsum = A("wsum", [128, NT], F32)
        gw_s = A("gw_s", [128, 2, 16], F32)
        gbB = A("gbB", [128, 16], F32)
        xf = A("xf", [128, 2, 256], F32)
        st6f = A("st6f", [128, 2, 6], F32)
        mvf = A("mvf", [128, 2, 2], F32)
        vef = A("vef", [128, 2], F32)
        rsf = A("rsf", [128, 2], F32)
        xnf = A("xnf", [128, 2, 256], F32)
        sl = A("sl", [128, 2, I], F32)
        ha = A("ha", [128, 2, I], F32)
        haT = A("haT", [128, 2, 2, 128], F32)
        yo = A("yo", [128, 2, 256], F32)

        for e in Q.ENGINES:
            Q.pause(e, done_a)
        xf_free = [None, None]

        def load_x1(i):
            return Q.add("sync", lambda e: e.dma_start(xf[:, i % 2], x1_d[128 * i:128 * i + 128, :]),
                         after=[xf_free[i % 2]], mark=f"l_x1{i % 2}", dma=True)

        load(gw_s[:, :, :], gw.rearrange("(k p) n -> p k n", p=128), "l_gw")
        t_gw = load(gbB[:, :], gbias.partition_broadcast(128), "l_gw")
        tx = {0: load_x1(0), 1: load_x1(1)}
        load(W13[:, 0], w13[0], "l_ew")
        load(W13[:, 1], w13[1], "l_ew")
        load(W2[:, :, 0, :], w2[0:128], "l_ew")
        t_ew = load(W2[0:64, :, 1, :], w2[128:192], "l_ew")
        tpf = [None] * 2
        xnf_free = [None, None]
        l_free = [None, None]
        for i in range(NT):
            b, s = i // 16, i % 2
            t = Q.add("vector", lambda e, s=s: e.bn_stats(st6f[:, s], xf[:, s]), after=[tx[i]], mark="ln2")
            t = Q.add("vector", lambda e, s=s: e.bn_aggr(mvf[:, s], st6f[:, s]), after=[t], mark="ln2")
            t = Q.add("vector", lambda e, s=s: e.tensor_scalar(vef[:, s:s + 1], mvf[:, s, 1:2], EPS, None, ALU.add),
                      after=[t], mark="ln2")
            t = Q.add("gpsimd", lambda e, s=s: e.tensor_tensor(rsf[:, s:s + 1], vef[:, s:s + 1], mhalf[:, 0:1], ALU.pow),
                      after=[t], mark="rs2")
            t = Q.add("vector", lambda e, s=s: e.tensor_scalar(
                xnf[:, s], xf[:, s], mvf[:, s, 0:1], rsf[:, s:s + 1], ALU.subtract, ALU.mult),
                after=[t, xnf_free[s]], mark="xn2")
            xf_free[s] = t
            if i + 2 < NT:
                tx[i + 2] = load_x1(i + 2)
            for f in (0, 1):
                tt = Q.add("tensor", lambda e, f=f, s=s: e.transpose(
                    PB[:, s, 128 * f:128 * f + 128], xnf[:, s, 128 * f:128 * f + 128], ident[:, :]),
                    after=[t, tpf[s]], mark="tp2")
            xnf_free[s] = tt
            for f in (0, 1):
                th = Q.add("scalar", lambda e, f=f, s=s, b=b, i=i: e.activation(
                    h2T[:, i, f, :], PB[:, s, 128 * f:128 * f + 128], ACT.Identity, bias=mT[:, 4 + f, b:b + 1],
                    scale=mT[:, 6 + f, b:b + 1]), after=[tt], mark="h2T")
            tpf[s] = th
            for f in (0, 1):
                tl = Q.add("tensor", lambda e, f=f, i=i: e.matmul(
                    PB[:, 2 + i // 32, 16 * (i % 32):16 * (i % 32) + 16], h2T[:, i, f, :], gw_s[:, f, :],
                    start=f == 0, stop=f == 1), after=[th, t_gw], mark="lg")
        t_h2 = th

        def vec(fn, after):
            return Q.add("vector", fn, after=after, mark="rt")

        lg = PB[:, 2:4, :].rearrange("p a (t e) -> p (a t) e", e=16)
        t = Q.add("scalar", lambda e: e.activation(sg[:, :, :], lg, ACT.Exp, scale=-1.0), after=[tl], mark="sge")
        t = vec(lambda e: e.tensor_scalar(rk[:, :, :], sg[:, :, :], 1.0, None, ALU.add), [t])
        t = vec(lambda e: e.reciprocal(sg[:, :, :], rk[:, :, :]), [t])
        t = vec(lambda e: e.tensor_tensor(sb_[:, :, :], sg[:, :, :], gbB[:, :].unsqueeze(1).broadcast_to([128, NT, 16]), ALU.add), [t, t_gw])
        m4 = sb_[:, :, :].rearrange("p t (g m) -> p t g m", m=4)
        first = True
        for a in range(4):
            for c in range(a + 1, 4):
                t = vec(lambda e, a=a, c=c, d=gs if first else gt: e.tensor_tensor(d[:, :, :], m4[:, :, :, a], m4[:, :, :, c], ALU.add), [t])
                if not first:
                    t = vec(lambda e: e.tensor_tensor(gs[:, :, :], gs[:, :, :], gt[:, :, :], ALU.max), [t])
                first = False
        t = vec(lambda e: e.memset(gr[:, :, :], 0.0), [t])
        t = vec(lambda e: e.memset(rk[:, :, :], 0.0), [t])

        def ranks(vals, rank, tmp, n, t):
            for d in range(1, n):
                lo = vals[:, :, 0:n - d]
                hi = vals[:, :, d:n]
                t = vec(lambda e, lo=lo, hi=hi, d=d: e.tensor_tensor(tmp[:, :, 0:n - d], lo, hi, ALU.is_ge), [t])
                t = vec(lambda e, d=d: e.tensor_tensor(rank[:, :, d:n], rank[:, :, d:n], tmp[:, :, 0:n - d], ALU.add), [t])
                t = vec(lambda e, d=d: e.tensor_tensor(rank[:, :, 0:n - d], rank[:, :, 0:n - d], tmp[:, :, 0:n - d], ALU.subtract), [t])
                t = vec(lambda e, d=d: e.tensor_scalar(rank[:, :, 0:n - d], rank[:, :, 0:n - d], 1.0, None, ALU.add), [t])
            return t

        t = ranks(gs, gr, gt, 4, t)
        t = vec(lambda e: e.tensor_scalar(gr[:, :, :], gr[:, :, :], 2.0, None, ALU.is_lt), [t])
        t = vec(lambda e: e.tensor_scalar(gt[:, :, :], gr[:, :, :], -1.0, BIG, ALU.add, ALU.mult), [t])
        t = vec(lambda e: e.tensor_tensor(m4, m4, gr[:, :, :].unsqueeze(3).broadcast_to([128, NT, 4, 4]), ALU.mult), [t])
        t = vec(lambda e: e.tensor_tensor(m4, m4, gt[:, :, :].unsqueeze(3).broadcast_to([128, NT, 4, 4]), ALU.add), [t])
        t = ranks(sb_, rk, cm, 16, t)
        t = vec(lambda e: e.tensor_scalar(rk[:, :, :], rk[:, :, :], 4.0, None, ALU.is_lt), [t])
        t = vec(lambda e: e.tensor_tensor(cm[:, :, :], rk[:, :, :], sg[:, :, :], ALU.mult), [t])
        t = vec(lambda e: e.tensor_reduce(wsum[:, :], cm[:, :, :], AX.X, ALU.add), [t])
        t = vec(lambda e: e.tensor_scalar(wsum[:, :], wsum[:, :], 1e-20, None, ALU.add), [t])
        t = vec(lambda e: e.reciprocal(wsum[:, :], wsum[:, :]), [t])
        t = vec(lambda e: e.tensor_tensor(cm[:, :, :], cm[:, :, :], wsum[:, :].unsqueeze(2).broadcast_to([128, NT, 16]), ALU.mult), [t])
        t_cm = vec(lambda e: e.tensor_scalar(cm[:, :, :], cm[:, :, :], 2.5, None, ALU.mult), [t])

        gu_free = [None] * 2
        sl_free = [None] * 2
        ha_free = [None] * 2
        ht_free = [None] * 2
        haT_free = [None] * 2
        y_free = [None] * 2
        yo_free = [None] * 2
        n = 0
        down = []
        for i in range(NT):
            b = i // 16
            tl = load_x1(i) if False else Q.add(
                "sync", lambda e, i=i: e.dma_start(xf[:, i % 2], x1_d[128 * i:128 * i + 128, :]),
                after=[xf_free[i % 2]], mark=f"l_x1{i % 2}", dma=True)
            for ex in range(NE):
                k, k3 = n % 2, n % 2
                n += 1
                for f in (0, 1):
                    t = Q.add("tensor", lambda e, i=i, f=f, ex=ex, k3=k3: e.matmul(
                        PB[:, k3, 0:2 * I], h2T[:, i, f, :], W13[:, f, ex, :], start=f == 0, stop=f == 1),
                        after=[t_h2, t_ew, gu_free[k3], t_cm], mark="gu")
                ts = Q.add("scalar", lambda e, k=k, k3=k3: e.activation(sl[:, k], PB[:, k3, 0:I], ACT.Silu),
                           after=[t, sl_free[k]], mark="sl")
                if ex < E:
                    tw = Q.add("vector", lambda e, i=i, ex=ex, k=k, k3=k3: e.scalar_tensor_tensor(
                        out=ha[:, k], in0=sl[:, k], scalar=cm[:, i, ex:ex + 1], in1=PB[:, k3, I:2 * I],
                        op0=ALU.mult, op1=ALU.mult), after=[ts, ha_free[k], t_cm], mark="ha")
                else:
                    tw = Q.add("vector", lambda e, k=k, k3=k3: e.tensor_tensor(
                        ha[:, k], sl[:, k], PB[:, k3, I:2 * I], ALU.mult), after=[ts, ha_free[k]], mark="ha")
                gu_free[k3] = sl_free[k] = tw

                def rest(i=i, ex=ex, k=k, tw=tw, b=b, tl=tl):
                    ba, bb = 2 + k, 4 + k
                    Q.add("tensor", lambda e: e.transpose(PB[:, ba, 0:128], ha[:, k, 0:128], ident[:, :]),
                          after=[tw, ht_free[k]], mark="ht")
                    tt = Q.add("tensor", lambda e: e.transpose(PB[0:64, bb, 0:128], ha[:, k, 128:192], ident[:, :]),
                               mark="ht")
                    ha_free[k] = tt
                    ta_ = Q.add("scalar", lambda e: e.activation(haT[:, k, 0, :], PB[:, ba, 0:128], ACT.Copy),
                                after=[tt, haT_free[k]], mark="haT_a")
                    tb_ = Q.add("vector", lambda e: e.tensor_copy(haT[0:64, k, 1, :], PB[0:64, bb, 0:128]),
                                after=[tt, haT_free[k]], mark="haT_b")
                    ht_free[k] = None

                    def dn():
                        yb = 6 + i % 2
                        Q.add("tensor", lambda e: e.matmul(PB[:, yb, 0:256], haT[:, k, 0, :], W2[:, ex, 0, :],
                                                           start=ex == 0, stop=False), after=[ta_, y_free[i % 2] if ex == 0 else None], mark="dn")
                        td = Q.add("tensor", lambda e: e.matmul(PB[:, yb, 0:256], haT[0:64, k, 1, :], W2[0:64, ex, 1, :],
                                                                start=False, stop=ex == NE - 1), after=[tb_], mark="dn")
                        haT_free[k] = td
                        if ex == NE - 1:
                            s = i % 2
                            ty = Q.add("vector", lambda e: e.tensor_tensor(yo[:, s], PB[:, yb, 0:256], GB[:, b], ALU.mult),
                                       after=[td, yo_free[s]], mark="yo")
                            y_free[s] = ty
                            ty = Q.add("vector", lambda e: e.tensor_tensor(yo[:, s], yo[:, s], xf[:, s], ALU.add),
                                       after=[ty, tl], mark="yo")
                            xf_free[s] = ty
                            yo_free[s] = Q.add("sync", lambda e: e.dma_start(out[128 * i:128 * i + 128, :], yo[:, s]),
                                               after=[ty], mark=f"w_o{s}", dma=True)
                    ht_free[k] = (ta_, tb_)
                    return dn
                down.append([2, rest])
                for x_ in list(down):
                    x_[0] -= 1
                    if x_[0] == 0:
                        down.remove(x_)
                        f_ = x_[1]()
                        if isinstance(f_, type(rest)) and f_ is not None:
                            down.append([1, f_])
        while down:
            for x_ in list(down):
                x_[0] -= 1
                if x_[0] <= 0:
                    down.remove(x_)
                    f_ = x_[1]()
                    if f_ is not None:
                        down.append([1, f_])
        Q.pause("sync", [(k, v) for k, v in Q.everything() if k.startswith("w_")])

        block = ctx.enter_context(nc.Block())

        @block.sync
        def _(eng):
            Q.play("sync", eng)

        @block.tensor
        def _(eng):
            Q.play("tensor", eng)

        @block.vector
        def _(eng):
            Q.play("vector", eng)

        @block.scalar
        def _(eng):
            Q.play("scalar", eng)

        @block.gpsimd
        def _(eng):
            Q.play("gpsimd", eng)


def tables():
    inv = (1.0 / (np.float32(10000.0) ** (np.arange(0, HD, 2, dtype=np.float32) / np.float32(HD)))).astype(np.float32)
    fr = np.arange(T, dtype=np.float32)[:, None] * inv[None, :]
    rope = np.concatenate([np.sin(fr.astype(np.float64)), np.cos(fr.astype(np.float64))], -1).astype(np.float32)
    s, c = rope[:, 0::2].T, rope[:, 1::2].T
    k = np.arange(128)
    cons = np.zeros((128, 4, 128), np.float32)
    cons[:, 0, :] = np.eye(128, dtype=np.float32)
    cons[:, 1, :] = k[:, None] == 32 * (k[None, :] // 32) + 16
    cons[:, 2, :] = np.where(k[None, :] > k[:, None], np.float32(-BIG), np.float32(0))
    cons[:, 3, :] = np.where(k[:, None] > k[None, :], np.float32(-BIG), np.float32(0))
    return np.ascontiguousarray(np.tile(c, (16, 1))), np.ascontiguousarray(np.tile(s, (16, 1))), cons


def kernel(L0_attn_x, L0_attn_qkv_w, L0_attn_qkv_b, L0_attn_out_w, L0_attn_out_b, L0_ffn_gate_w, L0_ffn_gate_bias,
           L0_ffn_w1, L0_ffn_w2, L0_ffn_w3, L0_ffn_ws1, L0_ffn_ws2, L0_ffn_ws3, L0_c, L0_wmod):
    import concourse.bacc as bacc
    from concourse.bass_utils import run_bass_kernel_spmd

    a = np.ascontiguousarray
    qkv_w, qkv_b = np.asarray(L0_attn_qkv_w), np.asarray(L0_attn_qkv_b)
    head = np.arange(H)[:, None] * HD
    cols = [(z * D + head + 2 * np.arange(8)[None, :] + o).reshape(-1) for z in (0, 1) for o in (0, 1)]
    wo = np.zeros((4, 4, 32, D), np.float32)
    wo[:, :, 0:HD, :] = np.asarray(L0_attn_out_w).reshape(4, 4, HD, D)
    w1 = np.concatenate([np.asarray(L0_ffn_w1), np.asarray(L0_ffn_ws1)[None]], 0)
    w3 = np.concatenate([np.asarray(L0_ffn_w3), np.asarray(L0_ffn_ws3)[None]], 0)
    w2 = np.concatenate([np.asarray(L0_ffn_w2), np.asarray(L0_ffn_ws2)[None]], 0)
    w13 = np.concatenate([w1, w3], 1).transpose(2, 0, 1).reshape(2, 128, NE, 2 * I)
    ropec, ropes, cons = tables()
    arrays = {
        "x": a(np.asarray(L0_attn_x).reshape(N, D)),
        "wqk": a(qkv_w[:, np.concatenate(cols)]),
        "wv": a(qkv_w[:, 2 * D:]),
        "bqk": a(np.stack([qkv_b[c] for c in cols], 1)),
        "bv": a(qkv_b[2 * D:]),
        "wo": a(wo.reshape(4, 128, D).transpose(1, 0, 2)),
        "ob": a(np.asarray(L0_attn_out_b)),
        "gw": a(np.asarray(L0_ffn_gate_w).T),
        "gbias": a(np.asarray(L0_ffn_gate_bias)),
        "w13": a(w13),
        "w2": a(w2.transpose(2, 0, 1)),
        "cT": a(np.asarray(L0_c).T.reshape(2, 128, B).transpose(1, 0, 2)),
        "wmod": a(np.asarray(L0_wmod)),
        "ropec": ropec,
        "ropes": ropes,
        "consts": cons,
    }
    nc = bacc.Bacc("TRN2", target_bir_lowering=False, num_devices=1)
    args = {n: nc.dram_tensor(f"in_{n}", v.shape, mybir.dt.from_np(v.dtype), kind="ExternalInput").ap()
            for n, v in arrays.items()}
    args["out"] = nc.dram_tensor("out_0", (N, D), F32, kind="ExternalOutput").ap()
    program(nc, **args)
    got = run_bass_kernel_spmd(nc, [{f"in_{n}": v for n, v in arrays.items()}], core_ids=[0])
    return got.results[0]["out_0"].reshape(B, T, D)
```

```python
from contextlib import ExitStack

import numpy as np

import concourse.bass as bass
from concourse import mybir

F32 = mybir.dt.float32
I32 = mybir.dt.int32
U32 = mybir.dt.uint32
BF16 = mybir.dt.bfloat16
ALU = mybir.AluOpType
ACT = mybir.ActivationFunctionType
AX = mybir.AxisListType

B, T, D, H, HD = 4, 2048, 256, 16, 16
N = B * T
NT = N // 128
E, I, G = 16, 192, 4
NE = E + 1
TOPK = 4
PARTS = 2
FIRST = (0, 48)
TILES = (48, 16)
NI = tuple(n * TOPK + E - 1 for n in TILES)
BIG = 1e30
EPS = 1e-5


class Queues:

    ENGINES = ("sync", "tensor", "vector", "scalar", "gpsimd")

    def __init__(self, nc, ctx):
        self.nc, self.ctx = nc, ctx
        self.q = {e: [] for e in self.ENGINES}
        self.sem, self.count = {}, {}

    def add(self, engine, fn, after=(), mark=None, dma=False):
        if mark is not None:
            if mark not in self.sem:
                self.sem[mark] = self.ctx.enter_context(self.nc.semaphore(mark))
                self.count[mark] = 0
            self.count[mark] += 16 if dma else 1
        flat = [x for t in after if t is not None for x in ([t] if isinstance(t[0], str) else t)]
        self.q[engine].append((fn, tuple(flat), mark, 16 if dma else 1))
        return None if mark is None else (mark, self.count[mark])

    def everything(self):
        return list(self.count.items())

    def pause(self, engine, tokens):
        self.q[engine].append((None, tuple(tokens), None, 0))

    def play(self, engine, eng):
        seen = {}
        for fn, after, mark, inc in self.q[engine]:
            for name, value in after:
                if seen.get(name, 0) < value:
                    eng.wait_ge(self.sem[name], value)
                    seen[name] = value
            if fn is None:
                continue
            ins = fn(eng)
            if mark is not None:
                ins.then_inc(self.sem[mark], inc)


class Arena:

    def __init__(self, nc, start):
        self.nc, self.at, self.n = nc, start, 0

    def __call__(self, name, shape, dt):
        size = int(np.prod(shape[1:])) * (2 if dt == BF16 else 4)
        size = (size + 31) // 32 * 32
        t = self.nc.alloc_sbuf_tensor_at(name, shape, dt, offset=self.at)
        self.at += size
        return t


def program(nc, x, wqk, wv, bqk, bv, wo, ob, gw, gbias, w13, w2, cT, wmod, ropec, ropes, consts, fconst, out):
    def scratch(name, shape, dt=F32):
        return nc.dram_tensor(name, shape, dt, kind="Internal").ap()

    parts_d = scratch("qk_parts", [B, H, 2, 3, HD, T], BF16)
    v_d = scratch("v_rows", [B, 4, 128, T // 128, 68])
    x1_d = scratch("x1_rows", [N, D])
    h2_d = scratch("h2_rows", [N, D])
    x2_d = scratch("x2_rows", [N, D])
    mod_d = scratch("mod_rows", [4, B, D])
    rd_d = scratch("rden_rows", [64, 4, 512])
    xg_d = [scratch(f"x_slots{p}", [(NI[p] + 1 + E) * 128, D]) for p in range(PARTS)]
    y_d = [scratch(f"y_slots{p}", [NI[p] * 128, D]) for p in range(PARTS)]

    with ExitStack() as ctx:
        Q = Queues(nc, ctx)
        PB = ctx.enter_context(nc.psum_tensor("PB", [128, 8, 512], F32))
        A = Arena(nc, (int(nc.sbuf_base) + 31) // 32 * 32)

        ident = A("ident", [128, 128], F32)
        identb = A("identb", [128, 128], BF16)
        m1 = A("m1", [128, 128], BF16)
        mhalf = A("mhalf", [128, 4], F32)
        mT = A("mT", [128, 4, 4], F32)
        obB = A("obB", [128, 256], F32)
        wo_s = A("wo_s", [128, 4, 256], F32)
        phase_start = A.at

        wm_s = A("wm_s", [128, 2, 1536], F32)
        cT_s = A("cT_s", [128, 2, 4], F32)
        ce = A("ce", [128, 2, 4], F32)
        cd = A("cd", [128, 2, 4], F32)
        cr = A("cr", [128, 2, 4], F32)
        sc = A("sc", [128, 2, 4], F32)
        scb = A("scb", [128, 2, 4, 128], F32)
        cons = A("cons", [128, 2, 128], F32)
        graw = A("graw", [1, 4, 4, 256], F32)
        gneg = A("gneg", [1, 4, 256], F32)
        gsg = A("gsg", [1, 4, 256], F32)
        wqk_s = A("wqk_s", [128, 2, 512], F32)
        wv_s = A("wv_s", [128, 2, 256], F32)
        bqk_s = A("bqk_s", [128, 4], F32)
        bvB = A("bvB", [128, 256], F32)
        rC = A("rC", [128, T], F32)
        rS = A("rS", [128, T], F32)
        xt = A("xt", [128, 2, 4, 256], F32)
        st6 = A("st6", [128, 2, 4, 6], F32)
        mv = A("mv", [128, 2, 4, 2], F32)
        ve = A("ve", [128, 2, 4], F32)
        rstd = A("rstd", [128, 2, 4], F32)
        xn = A("xn", [128, 2, 4, 256], F32)
        hT = A("hT", [128, 2, 2, 512], F32)
        ta = A("ta", [128, 2, 512], F32)
        tb = A("tb", [128, 2, 512], F32)
        r = A("r", [128, 2, 4, 512], F32)
        pe_ = A("pe_", [128, 2, 4, 512], F32)
        pt = A("pt", [128, 2, 3, 4, 512], BF16)
        vst = A("vst", [128, 2, 4, 4, 68], F32)

        def load(dst, src, mark, after=()):
            return Q.add("sync", lambda e: e.dma_start(dst, src), after=after, mark=mark, dma=True)

        load(cT_s[:, :, :], cT, "l_mod")
        load(cons[:, :, :], consts, "l_mod")
        t_mod = load(wm_s[:, :, :], wmod.rearrange("(k p) n -> p k n", p=128), "l_mod")
        xch = x.rearrange("(c t p) d -> c p t d", t=4, p=128)

        x_free = [None, None]
        tx = {}

        def load_x(c):
            tx[c] = load(xt[:, c % 2], xch[c], f"l_x{c % 2}", [x_free[c % 2]])

        load_x(0)
        load_x(1)
        load(wqk_s[:, :, :], wqk.rearrange("(k p) n -> p k n", p=128), "l_w")
        load(wv_s[:, :, :], wv.rearrange("(k p) n -> p k n", p=128), "l_w")
        load(bqk_s[:, :], bqk, "l_w")
        load(bvB[:, :], bv.partition_broadcast(128), "l_w")
        load(obB[:, :], ob.partition_broadcast(128), "l_w")
        load(wo_s[:, :, :], wo, "l_w")
        load(rC[:, :], ropec, "l_w")
        t_w = load(rS[:, :], ropes, "l_w")

        t = Q.add("scalar", lambda e: e.activation(ce[:, :, :], cT_s[:, :, :], ACT.Exp, scale=-1.0),
                  after=[t_mod], mark="c_exp")
        t = Q.add("vector", lambda e: e.tensor_scalar(cd[:, :, :], ce[:, :, :], 1.0, None, ALU.add), after=[t, t_mod], mark="c_v")
        t = Q.add("vector", lambda e: e.reciprocal(cr[:, :, :], cd[:, :, :]), after=[t], mark="c_v")
        t = t_sc = Q.add("vector", lambda e: e.tensor_tensor(sc[:, :, :], cT_s[:, :, :], cr[:, :, :], ALU.mult), after=[t], mark="c_v")
        Q.add("vector", lambda e: e.tensor_copy(ident[:, :], cons[:, 0, :]), mark="c_k")
        Q.add("vector", lambda e: e.tensor_copy(identb[:, :], cons[:, 0, :]), mark="c_k")
        Q.add("vector", lambda e: e.tensor_copy(m1[:, :], cons[:, 1, :]), mark="c_k")
        t_k = Q.add("vector", lambda e: e.memset(mhalf[:, :], -0.5), mark="c_k")
        Q.add("vector", lambda e: e.memset(vst[:, :, :, :, :], 1.0), mark="c_k")
        t_vst = ("c_k", Q.count["c_k"])

        for n, (kind, f) in enumerate([(k, f) for k in (0, 1) for f in (0, 1)]):
            for k in (0, 1):
                col = kind * 256 + f * 128
                t = Q.add("tensor", lambda e, n=n, k=k, col=col: e.matmul(
                    PB[:, 7, 4 * n:4 * n + 4], wm_s[:, k, col:col + 128], sc[:, k, :], start=k == 0, stop=k == 1),
                    after=[t_mod, t_sc], mark="m_mod")
        t = Q.add("vector", lambda e: e.tensor_copy(mT[:, :, :], PB[:, 7, 0:16].rearrange("p (n b) -> p n b", b=4)),
                  after=[t], mark="c_m")
        t_mT = Q.add("vector", lambda e: e.tensor_scalar(mT[:, 2:4, :], mT[:, 2:4, :], 1.0, None, ALU.add), after=[t], mark="c_m")
        t_gate = t_mT
        for n, kind in enumerate((2, 5, 3, 4)):
            for b in range(4):
                for k in (0, 1):
                    t = Q.add("tensor", lambda e, k=k, b=b, kind=kind, n=n: e.matmul(
                        PB[0:1, 3 + b // 2 + 2 * (n % 2), 256 * (b % 2):256 * (b % 2) + 256], sc[:, k, b:b + 1],
                        wm_s[:, k, kind * 256:kind * 256 + 256], start=k == 0, stop=k == 1), after=[t_gate], mark="m_gate")
            src = PB[0:1, 3 + 2 * (n % 2):5 + 2 * (n % 2), :].rearrange("p a (b d) -> p (a b) d", d=256)
            dst = graw[:, n]
            if n == 3:
                t = Q.add("vector", lambda e, dst=dst, src=src: e.tensor_scalar(dst, src, 1.0, None, ALU.add), after=[t], mark="c_g")
            else:
                t = Q.add("vector", lambda e, dst=dst, src=src: e.tensor_copy(dst, src), after=[t], mark="c_g")
            if n < 2:
                t = Q.add("vector", lambda e, dst=dst: e.tensor_scalar(gneg[:, :, :], dst, -1.0, None, ALU.mult), after=[t], mark="c_g")
                t = Q.add("vector", lambda e, dst=dst: e.tensor_scalar(gsg[:, :, :], dst, 0.0, 2.0, ALU.is_ge, ALU.mult), after=[t], mark="c_g")
                t = Q.add("vector", lambda e, dst=dst: e.tensor_tensor(gneg[:, :, :], dst, gneg[:, :, :], ALU.max), after=[t], mark="c_g")
                t = Q.add("vector", lambda e: e.tensor_scalar(gneg[:, :, :], gneg[:, :, :], 0.25, None, ALU.max), after=[t], mark="c_g")
                t = Q.add("vector", lambda e, dst=dst: e.scalar_tensor_tensor(
                    out=dst, in0=gsg[:, :, :], scalar=-1.0, in1=gneg[:, :, :], op0=ALU.add, op1=ALU.mult), after=[t], mark="c_g")
            t_gate = t
        t_modd = Q.add("sync", lambda e: e.dma_start(mod_d.rearrange("(o n) b d -> o n b d", o=1), graw[:, :, :, :]),
                       after=[t], mark="w_mod", dma=True)

        tp_free = [None, None]
        qk_free = [None] * 4
        v_free = [None] * 2
        hT_free = [None, None]
        r_free = [None, None]
        pe_free = [None, None]
        pt_free = [None, None]
        vst_free = [None, None]
        xn_free = [None, None]
        ro = [None, None]
        now = {}

        def p_norm(c):
            s = c % 2
            for i in range(4):
                t = Q.add("vector", lambda e, i=i: e.bn_stats(st6[:, s, i, :], xt[:, s, i, :]), after=[tx[c]], mark="ln")
            for i in range(4):
                t = Q.add("vector", lambda e, i=i: e.bn_aggr(mv[:, s, i, :], st6[:, s, i, :]), after=[t], mark="ln")
            t = Q.add("vector", lambda e: e.tensor_scalar(ve[:, s, :], mv[:, s, :, 1], EPS, None, ALU.add), after=[t], mark="ln")
            now["rs", c] = Q.add("gpsimd", lambda e: e.tensor_tensor(rstd[:, s, :], ve[:, s, :], mhalf[:, :], ALU.pow),
                                 after=[t, t_k], mark="rs")

        def p_rows(c):
            s, b = c % 2, c // 4
            for i in range(4):
                t = Q.add("vector", lambda e, i=i: e.tensor_scalar(
                    xn[:, s, i, :], xt[:, s, i, :], mv[:, s, i, 0:1], rstd[:, s, i:i + 1], ALU.subtract, ALU.mult),
                    after=[now["rs", c], xn_free[s]], mark="xn")
            x_free[s] = t
            if c + 2 < 16:
                load_x(c + 2)
            for f in (0, 1):
                for i in range(4):
                    tt = Q.add("tensor", lambda e, i=i, f=f: e.transpose(
                        PB[:, f, 128 * i:128 * i + 128], xn[:, s, i, 128 * f:128 * f + 128], ident[:, :]),
                        after=[t, t_k, tp_free[f]], mark="tp")
                th = Q.add("scalar", lambda e, f=f: e.activation(
                    hT[:, s, f, :], PB[:, f, :], ACT.Identity, bias=mT[:, f, b:b + 1], scale=mT[:, 2 + f, b:b + 1]),
                    after=[tt, t_mT, hT_free[s]], mark="hT")
                tp_free[f] = th
            xn_free[s] = tt
            now["hT", c] = th

        def p_qkv(c):
            s, b, tok = c % 2, c // 4, (c % 4) * 512
            th = now["hT", c]
            for z in (0, 1):
                tq = []
                for m in (2 * z, 2 * z + 1):
                    for f in (0, 1):
                        t = Q.add("tensor", lambda e, m=m, f=f: e.matmul(
                            PB[:, 2 + m, :], wqk_s[:, f, 128 * m:128 * m + 128], hT[:, s, f, :], start=f == 0, stop=f == 1),
                            after=[th, t_w, qk_free[m], t_gate], mark="qk")
                    tq.append(t)
                lo, hi = 2 + 2 * z, 3 + 2 * z
                C, S = rC[:, tok:tok + 512], rS[:, tok:tok + 512]

                def rot(dst, bank, tab):
                    return lambda e: e.scalar_tensor_tensor(out=dst, in0=PB[:, bank, :], scalar=bqk_s[:, bank - 2:bank - 1],
                                                            in1=tab, op0=ALU.add, op1=ALU.mult)
                for half, (tl, th_, op) in enumerate(((C, S, ALU.subtract), (S, C, ALU.add))):
                    Q.add("vector", rot(ta[:, half], lo, tl), after=[tq[0], ro[half]], mark="rot")
                    t = Q.add("vector", rot(tb[:, half], hi, th_), after=[tq[1]], mark="rot")
                    ro[half] = Q.add("gpsimd", lambda e, half=half, z=z, op=op: e.tensor_tensor(
                        r[:, s, 2 * z + half, :], ta[:, half], tb[:, half], op), after=[t, r_free[s]], mark="rsum")
                qk_free[2 * z] = qk_free[2 * z + 1] = t
            for m in range(2):
                for i in (2 * m, 2 * m + 1):
                    for f in (0, 1):
                        t = Q.add("tensor", lambda e, m=m, i=i, f=f: e.matmul(
                            PB[:, 6 + m, 256 * (i % 2):256 * (i % 2) + 256], hT[:, s, f, 128 * i:128 * i + 128],
                            wv_s[:, f, :], start=f == 0, stop=f == 1), after=[th, v_free[m]], mark="v")
                for i in (2 * m, 2 * m + 1):
                    v_free[m] = Q.add("vector", lambda e, m=m, i=i: e.tensor_tensor(
                        vst[:, s, :, i, :].rearrange("p g (h d) -> p g h d", d=17)[:, :, :, 0:16],
                        PB[:, 6 + m, 256 * (i % 2):256 * (i % 2) + 256].rearrange("p (g h d) -> p g h d", g=4, d=16),
                        bvB[:, :].rearrange("p (g h d) -> p g h d", g=4, d=16), ALU.add),
                        after=[t, vst_free[s], t_w, t_vst], mark="vb")
            hT_free[s] = t
            vst_free[s] = Q.add("sync", lambda e: e.dma_start(
                v_d[b].rearrange("g p t e -> p g t e")[:, :, 4 * (c % 4):4 * (c % 4) + 4, :], vst[:, s]),
                after=[v_free[1]], mark=f"w_v{s}", dma=True)
            now["r", c] = ro[1]

        def p_hi(c):
            s = c % 2
            t = Q.add("scalar", lambda e: e.activation(pt[:, s, 0], r[:, s], ACT.Copy), after=[now["r", c], pt_free[s]], mark="p_hi")
            r_free[s] = now["rest", c] = Q.add("gpsimd", lambda e: e.tensor_tensor(pe_[:, s], r[:, s], pt[:, s, 0], ALU.subtract),
                                               after=[t, pe_free[s]], mark="p_rest")

        def p_lo(c):
            s, b, tok = c % 2, c // 4, (c % 4) * 512
            t = Q.add("scalar", lambda e: e.activation(pt[:, s, 1], pe_[:, s], ACT.Copy), after=[now["rest", c]], mark="p_mid")
            t = pe_free[s] = Q.add("vector", lambda e: e.tensor_tensor(pt[:, s, 2], pe_[:, s], pt[:, s, 1], ALU.subtract),
                                   after=[t], mark="p_lo")
            for z in (0, 1):
                for k in range(3):
                    for half in (0, 1):
                        dst = parts_d[b, :, z, k, 8 * half:8 * half + 8, tok:tok + 512]
                        pt_free[s] = Q.add("sync", lambda e, k=k, z=z, half=half, dst=dst: e.dma_start(
                            dst, pt[:, s, k, 2 * z + half, :]), after=[t], mark=f"w_p{s}", dma=True)

        stages = (p_norm, p_rows, p_qkv, p_hi, p_lo)
        for it in range(16 + len(stages) - 1):
            for d in reversed(range(len(stages))):
                if 0 <= it - d < 16:
                    stages[d](it - d)

        done_p = Q.everything()

        A.at = phase_start
        L = A("L", [128, NT, 16], F32)
        sidu = A("sidu", [128, NT, 4], U32)
        wts = A("wts", [128, NT, 4], F32)
        tile_e = [A(f"tile_e{p}", [1, NI[p] + 1], I32) for p in range(PARTS)]
        gw_s = A("gw_s", [128, 2, 16], F32)
        gbB = A("gbB", [128, 16], F32)
        FC = 48 + NI[0] + 1 + 1 + 2 * E
        fc_s = A("fc_s", [128, FC], F32)
        osb = A("osb", [128, 2, 512], F32)
        d16 = A("d16", [128, 2, 16], F32)
        r16 = A("r16", [128, 2, 16], F32)
        rden = A("rden", [128, 2, 512], F32)
        mx = A("mx", [128, 4, 16, 4], F32)
        nm = A("nm", [128, 4, 16], F32)
        nh = A("nh", [16, 2, 2, 128], BF16)
        XI = 6
        xin = A("xin", [128, XI, 256], F32)
        xo = A("xo", [128, 2, 256], F32)
        h2t = A("h2t", [128, 3, 256], F32)
        lT = A("lT", [128, 2, 128], F32)
        gaB = A("gaB", [128, 256], F32)
        modB = A("modB", [128, 2, 256], F32)
        st6f = A("st6f", [128, 2, 6], F32)
        mvf = A("mvf", [128, 2, 2], F32)
        vef = A("vef", [128, 2], F32)
        rsf = A("rsf", [128, 2], F32)
        on_at = A.at
        ON = A("ON", [128, 4, T], F32)
        route_at = A.at
        QO = A("QO", [98, 3, 4, T], BF16)
        ffn_at = route_at + 2 * 4 * T * 2
        KO = A("KO", [98, 3, 4, T], BF16)
        V = A("V", [128, 3, 16, 68], F32)
        NP = 5
        P = A("P", [128, NP, 2, 512], F32)

        for e in Q.ENGINES:
            Q.pause(e, done_p)
        t_mx = Q.add("vector", lambda e: e.memset(mx[:, :, :, :], -3.0e38), mark="a_mx")
        t_ones = Q.add("gpsimd", lambda e: e.memset(KO[96:98, :, :, :], 1.0), mark="a_ones")
        t_o0 = Q.add("vector", lambda e: e.memset(PB[:, 7, :], 0.0), mark="a_o0")
        Q.pause("vector", [t_mx, t_o0])

        def load_g(g, after):
            b, h0, s = g // 4, 4 * (g % 4), (g + 2) % 3
            for dst, z, plan in ((QO, 0, ((0, 0, 3), (48, 0, 2), (80, 0, 1))),
                                 (KO, 1, ((0, 0, 1), (16, 0, 1), (32, 0, 1), (48, 1, 1), (64, 1, 1), (80, 2, 1)))):
                for row, k, n in plan:
                    load(dst[row:row + 16 * n, s], parts_d[b, h0:h0 + 4, z, k:k + n].rearrange("h k d t -> (k d) h t"), f"l_g{s}", after)
            return load(V[:, s], v_d[b, g % 4], f"l_g{s}", after)

        units = [0]
        unit_read = []
        unit_banks = [4, 5, 6]
        bank7 = [None]

        def unit_bank():
            u = units[0]
            units[0] += 1
            if len(unit_banks) == 1:
                return 7, bank7[0] if bank7[0] is not None else unit_read[u - 1]
            n = len(unit_banks)
            return unit_banks[u % n], unit_read[u - n] if u >= n else None

        def unit_done(t):
            unit_read.append(t)
            if len(unit_banks) == 1:
                bank7[0] = None

        nm_dma = {}
        loaded = {}

        def max_units(g):
            s = (g + 2) % 3
            for j in range(4):
                for t in range(16):
                    n_all = 128 * (t + 1)
                    for kc in range((n_all + 511) // 512):
                        def emit(j=j, t=t, kc=kc, n=min(512, n_all - 512 * kc), last=512 * kc + 512 >= n_all):
                            bank, free = unit_bank()
                            tk = Q.add("tensor", lambda e: e.matmul(
                                PB[:, bank, 0:n], QO[0:96, s, j, 128 * t:128 * t + 128],
                                KO[0:96, s, j, 512 * kc:512 * kc + n], start=True, stop=True),
                                after=[loaded[g], free], mark="s")
                            if last:
                                tk = Q.add("tensor", lambda e: e.matmul(
                                    PB[:, bank, n - 128:n], identb[:, :], m1[:, :], start=False, stop=True,
                                    skip_group_check=True), mark="s")
                            unit_done(Q.add("vector", lambda e: e.tensor_reduce(
                                mx[:, j, t, kc:kc + 1], PB[:, bank, 0:n], AX.X, ALU.max), after=[tk], mark="mx"))
                        yield emit

                def fin(j=j):
                    now["nm"] = Q.add("vector", lambda e: e.tensor_reduce(nm[:, j, :], mx[:, j], AX.X, ALU.max, negate=True),
                                      after=[unit_read[-1]], mark="nm")
                yield fin

                def turn(j=j):
                    bank, free = unit_bank()
                    tk = Q.add("tensor", lambda e: e.transpose(PB[0:16, bank, 0:128], nm[:, j, :], ident[:, :]),
                               after=[now["nm"], free], mark="s")
                    tk = Q.add("vector", lambda e: e.tensor_copy(nh[:, j % 2, 0, :], PB[0:16, bank, 0:128]),
                               after=[tk, nm_dma.get((g, j - 2) if j > 1 else (g - 1, j + 2))], mark="nh")
                    tk = Q.add("vector", lambda e: e.tensor_tensor(nh[:, j % 2, 1, :], PB[0:16, bank, 0:128], nh[:, j % 2, 0, :],
                                                                   ALU.subtract), after=[tk], mark="mx")
                    unit_done(tk)
                    for k in (0, 1):
                        nm_dma[g, j] = Q.add("gpsimd", lambda e, k=k: e.dma_start(
                            QO[96 + k:97 + k, s, j, :].rearrange("o (t q) -> o t q", q=128),
                            nh[:, j % 2, k, :]), after=[tk, loaded[g]], mark=f"w_nm{j}", dma=True)
                yield turn

        on_tok = {}
        proj_tok = {}
        xin_free = [None] * XI
        xo_free = [None] * 2
        h2_free = [None] * 3
        lT_free = [None]
        modB_free = [None]
        gaB_free = [None]
        x1_tok, h2_tok, l_tok = {}, {}, {}

        t_rt = load(gw_s[:, :, :], gw.rearrange("(k p) n -> p k n", p=128), "l_rt")
        t_rt = load(fc_s[:, :], fconst, "l_rt")
        t_rt = load(gbB[:, :], gbias.partition_broadcast(128), "l_rt")

        def o_load(b, t):
            i = 16 * b + t
            if t == 0:
                now["ga", b] = load(gaB[:, :], mod_d[0, b].partition_broadcast(128), "l_ga", [gaB_free[0]])
                now["mod", b] = load(modB[:, :, :], mod_d[2:4, b].partition_broadcast(128), "l_mb", [modB_free[0]])
            now["xi", i] = load(xin[:, i % XI], x[128 * i:128 * i + 128, :], f"l_xi{i % XI}", [xin_free[i % XI]])

        def o_proj(b, t):
            i = 16 * b + t
            bank, free = unit_bank()
            for gi in range(4):
                tk = Q.add("tensor", lambda e, gi=gi: e.matmul(
                    PB[:, bank, 0:256], ON[:, gi, 128 * t:128 * t + 128], wo_s[:, gi, :], start=gi == 0, stop=gi == 3),
                    after=[free, on_tok[b, 3, t // 4]], mark="s")
            proj_tok[b, t] = tk
            now["xo", i] = Q.add("vector", lambda e: e.tensor_tensor(xo[:, i % 2], PB[:, bank, 0:256], obB[:, :], ALU.add),
                                 after=[tk, xo_free[i % 2]], mark="xo")
            unit_done(now["xo", i])

        def o_x1(b, t):
            i = 16 * b + t
            tk = Q.add("gpsimd", lambda e: e.tensor_tensor(xo[:, i % 2], xo[:, i % 2], gaB[:, :], ALU.mult),
                       after=[now["xo", i], now["ga", b]], mark="xg")
            gaB_free[0] = tk
            tk = Q.add("gpsimd", lambda e: e.tensor_tensor(xin[:, i % XI], xo[:, i % 2], xin[:, i % XI], ALU.add),
                       after=[tk, now["xi", i]], mark="x1")
            xo_free[i % 2] = now["x1", i] = tk
            x1_tok[i] = Q.add("sync", lambda e: e.dma_start(x1_d[128 * i:128 * i + 128, :], xin[:, i % XI]), after=[tk],
                              mark=f"w_x1{i % XI}", dma=True)

        def o_stat(b, t):
            i = 16 * b + t
            k = i % 2
            tk = Q.add("vector", lambda e: e.bn_stats(st6f[:, k], xin[:, i % XI]), after=[now["x1", i]], mark="ln2")
            tk = Q.add("vector", lambda e: e.bn_aggr(mvf[:, k], st6f[:, k]), after=[tk, now.get(("xn2", i - 2))], mark="ln2")
            tk = Q.add("vector", lambda e: e.tensor_scalar(vef[:, k:k + 1], mvf[:, k, 1:2], EPS, None, ALU.add), after=[tk, now.get(("rs2", i - 2))], mark="ln2")
            now["rs2", i] = Q.add("gpsimd", lambda e: e.tensor_tensor(rsf[:, k:k + 1], vef[:, k:k + 1], mhalf[:, 0:1], ALU.pow),
                                  after=[tk, now.get(("xn2", i - 2))], mark="rs2")

        def o_h2(b, t):
            i = 16 * b + t
            k, k3 = i % 2, i % 3
            tk = Q.add("vector", lambda e: e.tensor_scalar(
                h2t[:, k3], xin[:, i % XI], mvf[:, k, 0:1], rsf[:, k:k + 1], ALU.subtract, ALU.mult),
                after=[now["rs2", i], h2_free[k3]], mark="xn2")
            now["xn2", i] = tk
            xin_free[i % XI] = (tk, x1_tok[i])
            tk = Q.add("gpsimd", lambda e: e.tensor_tensor(h2t[:, k3], h2t[:, k3], modB[:, 1], ALU.mult), after=[tk, now["mod", b]], mark="md2")
            tk = Q.add("gpsimd", lambda e: e.tensor_tensor(h2t[:, k3], h2t[:, k3], modB[:, 0], ALU.add), after=[tk], mark="md2")
            modB_free[0] = now["h2", i] = tk
            h2_tok[i] = Q.add("sync", lambda e: e.dma_start(h2_d[128 * i:128 * i + 128, :], h2t[:, k3]), after=[tk],
                              mark=f"w_h2{k3}", dma=True)

        def o_turn(b, t):
            i = 16 * b + t
            bank, free = unit_bank()
            for f in (0, 1):
                tk = Q.add("tensor", lambda e, f=f: e.transpose(
                    PB[:, bank, 128 * f:128 * f + 128], h2t[:, i % 3, 128 * f:128 * f + 128], ident[:, :]),
                    after=[now["h2", i], free], mark="s")
            h2_free[i % 3] = (tk, h2_tok[i])
            now["lT", i] = Q.add("scalar", lambda e: e.activation(
                lT[:, :, :], PB[:, bank, 0:256].rearrange("p (f q) -> p f q", f=2), ACT.Copy), after=[tk, lT_free[0]], mark="lT")
            unit_done(now["lT", i])

        def o_logits(b, t):
            i = 16 * b + t
            bank, free = unit_bank()
            for f in (0, 1):
                tk = Q.add("tensor", lambda e, f=f: e.matmul(PB[:, bank, 0:16], lT[:, f, :], gw_s[:, f, :],
                                                             start=f == 0, stop=f == 1), after=[now["lT", i], t_rt, free], mark="s")
            lT_free[0] = tk
            l_tok[i] = Q.add("vector", lambda e: e.tensor_copy(L[:, i, :], PB[:, bank, 0:16]), after=[tk], mark="L")
            unit_done(l_tok[i])

        o_stages = (o_load, None, o_proj, o_x1, o_stat, o_h2, o_turn, o_logits)

        def project(b):
            for it in range(16 + len(o_stages) - 1):
                for d in reversed(range(len(o_stages))):
                    if 0 <= it - d < 16 and o_stages[d] is not None:
                        o_stages[d](b, it - d)
                        yield

        st_read = [None, None]
        p_read = [None] * NP
        np_ = [0]
        o_free = [t_o0]
        osb_free = [None, None]
        d16_free = [None, None]
        r16_free = [None, None]
        rd_free = [None, None]
        nchunk = [0]
        done_g = {}
        pend = []
        late = []

        def tick(n=1):
            for _ in range(n):
                for x_ in list(late):
                    x_[0] -= 1
                    if x_[0] <= 0:
                        late.remove(x_)
                        x_[1]()

        def st_one(g, p, c, kt, jj, pb):
            s, j = (g + 2) % 3, 2 * p + jj
            q0 = max(c * 512, kt * 128)
            n = (c + 1) * 512 - q0
            diag = kt >= 4 * c
            tk = Q.add("tensor", lambda e: e.matmul(
                PB[:, j, 0:n], KO[0:98, s, j, 128 * kt:128 * kt + 128], QO[0:98, s, j, q0:q0 + n],
                start=True, stop=True), after=[loaded[g], nm_dma[g, j], t_ones, st_read[p]], mark="st")
            if jj == 0:
                return None
            te = st_read[p] = Q.add("scalar", lambda e: e.activation(
                P[:, pb, :, 0:n], PB[:, 2 * p:2 * p + 2, 0:n], ACT.Exp, scale=0.25), after=[tk, p_read[pb]], mark="exp")
            if diag:
                te = Q.add("gpsimd", lambda e: e.affine_select(
                    out=P[:, pb, :, 0:128], in_=P[:, pb, :, 0:128], compare_op=ALU.is_ge, fill=0.0, base=0,
                    pattern=[[0, 2], [1, 128]], channel_multiplier=-1), after=[te], mark="cut")
            return pb, te, q0 - c * 512, n

        def pv(g, c, kt, pair):
            b, gi, s = g // 4, g % 4, (g + 2) % 3
            ch = nchunk[0]
            ob_ = ch % 2
            for j in range(4):
                pb, te, o0, n = pair[j // 2]
                tk = Q.add("tensor", lambda e, j=j, pb=pb, o0=o0, n=n: e.matmul(
                    PB[32 * j:32 * j + 17, 7, o0:512], V[:, s, kt, 17 * j:17 * j + 17], P[:, pb, j % 2, 0:n],
                    start=kt == 0, stop=True, skip_group_check=True),
                    after=[pair[0][1], pair[1][1], o_free[0] if kt == 0 else None], mark="pv")
            for pb, *_ in pair:
                p_read[pb] = tk
            if kt < 4 * c + 3:
                return tk
            nchunk[0] += 1
            toc = o_free[0] = Q.add("scalar", lambda e: e.activation(osb[:, ob_], PB[:, 7, :], ACT.Copy),
                                    after=[tk, osb_free[ob_]], mark="oc")
            t1 = load(d16[:, ob_, :], osb[16:113:32, ob_, :].rearrange("p (a f) -> p a f", f=16), f"l_d{ob_}", [toc, d16_free[ob_]])

            def invert():
                t2 = d16_free[ob_] = Q.add("vector", lambda e: e.reciprocal(r16[:, ob_, :], d16[:, ob_, :]),
                                           after=[t1, r16_free[ob_]], mark="rd")
                t3 = r16_free[ob_] = Q.add("sync", lambda e: e.dma_start(
                    rd_d[ch].rearrange("j (a f) -> (j a) f", f=16), r16[:, ob_, :]), after=[t2], mark=f"w_rd{ob_}", dma=True)
                for j in range(4):
                    t4 = load(rden[32 * j:32 * j + 32, ob_, :], rd_d[ch, j].partition_broadcast(32), f"l_rd{ob_}", [t3, rd_free[ob_]])
                now["rd", ch] = t4

            def norm():
                need = [proj_tok[b - 1, 4 * c + i] for i in range(4)] if b > 0 else []
                ton = Q.add("gpsimd", lambda e: e.tensor_tensor(
                    ON[:, gi, 512 * c:512 * c + 512], osb[:, ob_], rden[:, ob_], ALU.mult), after=[now["rd", ch], toc, *need], mark="on")
                osb_free[ob_] = rd_free[ob_] = ton
                on_tok[b, gi, c] = ton
            late.append([4, invert])
            late.append([8, norm])
            return tk

        def group(g, pump):
            mu = list(max_units(g + 1)) if g < 15 else []
            done = [0]

            def unit(limit):
                if done[0] < min(limit, len(mu)):
                    mu[done[0]]()
                    done[0] += 1

            for i, (c, kt) in enumerate([(c, kt) for c in range(4) for kt in range(4 * c + 4)]):
                want = min(len(mu), -(-len(mu) * (i + 1) // 38))
                pbs = [(np_[0] + k) % NP for k in (0, 1)]
                np_[0] += 2
                st_one(g, 0, c, kt, 0, pbs[0])
                unit(want)
                p0 = st_one(g, 0, c, kt, 1, pbs[0])
                unit(want)
                if len(pend) == 2:
                    g_, *rest = pend.pop(0)
                    done_g[g_] = pv(g_, *rest)
                unit(want)
                st_one(g, 1, c, kt, 0, pbs[1])
                unit(want)
                p1 = st_one(g, 1, c, kt, 1, pbs[1])
                while done[0] < want:
                    unit(want)
                pend.append((g, c, kt, (p0, p1)))
                if i >= 2:
                    for f, rate in pump:
                        for _ in range(rate):
                            next(f, None)
                tick()
                if i == 9 and 0 < g and g + 2 < 16:
                    loaded[g + 2] = load_g(g + 2, [done_g[g - 1]])

        for g in range(3):
            loaded[g] = load_g(g, [])
        for emit in max_units(0):
            emit()

        def route_space():
            now["space"] = A.at
            A.at = route_at
            PT = TILES[0]
            R = {n: A(n, [128, PT, 16], F32) for n in ("sg", "sb_", "rk", "cm", "slot", "sa")}
            R["selb"] = A("selb", [128, PT, 16], BF16)
            R.update({n: A(n, [128, PT, 4], F32) for n in ("gs", "gt", "gr")})
            R["wsum"] = A("wsum", [128, PT], F32)
            R.update({n: A(n, [128, 16], F32) for n in ("cnt", "ntile", "zidx", "zpad")})
            R["cend"] = A("cend", [128, 2, 16], F32)
            R.update({n: A(n, [1, NI[0] + 1], F32) for n in ("tie", "tic")})
            R["zr"] = A("zr", [128, 256], F32)
            R["zidu"] = A("zidu", [128, PARTS, 16], U32)
            R["utri"] = A("utri", [128, 128], BF16)
            R["onesb"] = A("onesb", [128, 128], BF16)
            R["hs"] = A("hs", [128, 3, 256], F32)
            assert A.at <= ffn_at, A.at - ffn_at
            A.at = now["space"]
            return R

        R = route_space()
        ready = {}
        t_tail = {}
        hs_free = [None] * 3
        hs_n = [0]

        def route(p):
            T0, PT = FIRST[p], TILES[p]
            sg, sb_, rk, cm, slot, sa, selb, gs, gt, gr = (R[n][:, 0:PT, :] for n in ("sg", "sb_", "rk", "cm", "slot", "sa", "selb", "gs", "gt", "gr"))
            wsum = R["wsum"][:, 0:PT]
            cnt, ntile, zidx, zpad = (R[n][:, :] for n in ("cnt", "ntile", "zidx", "zpad"))
            cend = R["cend"]
            n_i = NI[p] + 1
            tie, tic = R["tie"][:, 0:n_i], R["tic"][:, 0:n_i]
            k128, tix = fc_s[:, 0:PT], fc_s[0:1, 48:48 + n_i]
            o = 48 + NI[0] + 1
            iotas, spare = fc_s[:, o:o + 1], fc_s[:, o + 1 + E * p:o + 1 + E * p + E]
            if p == 0:
                ready["zr"] = Q.add("gpsimd", lambda e: e.memset(R["zr"][:, :], 0.0), after=[done_g[14]], mark="f_z")
                t_on = Q.add("gpsimd", lambda e: e.memset(R["onesb"][:, :], 1.0), mark="f_o")
                ready["ut"] = Q.add("gpsimd", lambda e: e.affine_select(
                    out=R["utri"][:, :], in_=R["onesb"][:, :], compare_op=ALU.is_gt, fill=0.0, base=0, pattern=[[1, 128]],
                    channel_multiplier=-1), after=[t_on], mark="f_u")
                for q in range(PARTS):
                    for z in range(TILES[q] * TOPK, NI[q] + 1):
                        t_tail[q] = Q.add("sync", lambda e, q=q, z=z: e.dma_start(xg_d[q][128 * z:128 * z + 128, :], R["zr"][:, :]),
                                          after=[ready["zr"]], mark=f"w_t{q}", dma=True)
            last = [(l_tok[T0 + PT - 1], done_g[14], *([ready["rt", p - 1]] if p else []))]

            def vec(fn, *more):
                last[0] = Q.add("vector", fn, after=[last[0], *more], mark="rt")

            last[0] = Q.add("scalar", lambda e: e.activation(sg, L[:, T0:T0 + PT, :], ACT.Exp, scale=-1.0),
                            after=[last[0]], mark="sge")
            vec(lambda e: e.tensor_scalar(rk, sg, 1.0, None, ALU.add))
            vec(lambda e: e.reciprocal(sg, rk))
            yield
            vec(lambda e: e.tensor_tensor(sb_, sg, gbB[:, :].unsqueeze(1).broadcast_to([128, PT, 16]), ALU.add), t_rt)
            m4 = sb_.rearrange("p t (g m) -> p t g m", m=4)
            first = True
            for a in range(4):
                for c in range(a + 1, 4):
                    vec(lambda e, a=a, c=c, d=gs if first else gt: e.tensor_tensor(d, m4[:, :, :, a], m4[:, :, :, c], ALU.add))
                    if not first:
                        vec(lambda e: e.tensor_tensor(gs, gs, gt, ALU.max))
                    first = False
                    yield
            vec(lambda e: e.memset(gr, 0.0))
            vec(lambda e: e.memset(rk, 0.0))

            def ranks(vals, rank, tmp, n):
                for d in range(1, n):
                    lo, hi = vals[:, :, 0:n - d], vals[:, :, d:n]
                    vec(lambda e, lo=lo, hi=hi, d=d: e.tensor_tensor(tmp[:, :, 0:n - d], lo, hi, ALU.is_ge))
                    vec(lambda e, d=d: e.tensor_tensor(rank[:, :, d:n], rank[:, :, d:n], tmp[:, :, 0:n - d], ALU.add))
                    vec(lambda e, d=d: e.scalar_tensor_tensor(
                        out=rank[:, :, 0:n - d], in0=rank[:, :, 0:n - d], scalar=1.0, in1=tmp[:, :, 0:n - d],
                        op0=ALU.add, op1=ALU.subtract))
                    yield

            yield from ranks(gs, gr, gt, 4)
            vec(lambda e: e.tensor_scalar(gr, gr, 2.0, None, ALU.is_lt))
            vec(lambda e: e.tensor_scalar(gt, gr, -1.0, BIG, ALU.add, ALU.mult))
            vec(lambda e: e.tensor_tensor(m4, m4, gr.unsqueeze(3).broadcast_to([128, PT, 4, 4]), ALU.mult))
            vec(lambda e: e.tensor_tensor(m4, m4, gt.unsqueeze(3).broadcast_to([128, PT, 4, 4]), ALU.add))
            yield
            yield from ranks(sb_, rk, cm, 16)
            vec(lambda e: e.tensor_scalar(selb, rk, 4.0, None, ALU.is_lt))
            t_sel = last[0]
            vec(lambda e: e.tensor_tensor(cm, selb, sg, ALU.mult))
            vec(lambda e: e.tensor_reduce(wsum, cm, AX.X, ALU.add))
            vec(lambda e: e.tensor_scalar(wsum, wsum, 1e-20, None, ALU.add))
            vec(lambda e: e.reciprocal(wsum, wsum))
            vec(lambda e: e.tensor_tensor(cm, cm, wsum.unsqueeze(2).broadcast_to([128, PT, 16]), ALU.mult))
            vec(lambda e: e.tensor_scalar(cm, cm, 2.5, None, ALU.mult))
            yield
            for lo in range(0, PT, 24):
                n = min(24, PT - lo)
                for mat, dst in ((R["onesb"], sa), (R["utri"], slot)):
                    bank, free = unit_bank()
                    tk = Q.add("tensor", lambda e, lo=lo, n=n, mat=mat, bank=bank: e.matmul(
                        PB[:, bank, 0:16 * n], mat[:, :], selb[:, lo:lo + n, :].rearrange("p t e -> p (t e)"), start=True, stop=True),
                        after=[t_sel, ready["ut"], free], mark="s")
                    vec(lambda e, lo=lo, n=n, dst=dst, bank=bank: e.tensor_copy(
                        dst[:, lo:lo + n, :], PB[:, bank, 0:16 * n].rearrange("p (t e) -> p t e", e=16)), tk)
                    unit_done(last[0])
                    yield
            vec(lambda e: e.tensor_tensor(slot, slot, sa, ALU.subtract))
            bufs = [sa, sb_]
            d = 1
            while d < PT:
                a_, b_ = bufs
                vec(lambda e, a_=a_, b_=b_, d=d: e.tensor_copy(b_[:, 0:d, :], a_[:, 0:d, :]))
                vec(lambda e, a_=a_, b_=b_, d=d: e.tensor_tensor(b_[:, d:PT, :], a_[:, d:PT, :], a_[:, 0:PT - d, :], ALU.add))
                bufs = [b_, a_]
                d *= 2
                yield
            inc, other = bufs
            vec(lambda e: e.tensor_tensor(slot, slot, inc, ALU.add))
            vec(lambda e: e.tensor_copy(cnt, inc[:, PT - 1, :]))
            ticmp = other.rearrange("p t e -> p (t e)").rearrange("p (e t) -> p e t", e=16)
            vec(lambda e: e.tensor_tensor(ticmp, cnt.unsqueeze(2).broadcast_to([128, 16, PT]),
                                          k128.unsqueeze(1).broadcast_to([128, 16, PT]), ALU.is_gt), t_rt)
            vec(lambda e: e.tensor_reduce(ntile, ticmp, AX.X, ALU.add))
            yield
            vec(lambda e: e.tensor_copy(cend[:, 0, :], ntile))
            cur, d = 0, 1
            while d < 16:
                vec(lambda e, cur=cur, d=d: e.tensor_copy(cend[:, 1 - cur, 0:d], cend[:, cur, 0:d]))
                vec(lambda e, cur=cur, d=d: e.tensor_tensor(cend[:, 1 - cur, d:16], cend[:, cur, d:16], cend[:, cur, 0:16 - d], ALU.add))
                cur, d = 1 - cur, 2 * d
            ce_, base = cend[:, cur, :], cend[:, 1 - cur, :]
            vec(lambda e: e.tensor_tensor(base, ce_, ntile, ALU.subtract))
            vec(lambda e: e.tensor_scalar(base, base, 128.0, None, ALU.mult))
            yield
            vec(lambda e: e.tensor_tensor(slot, slot, base.unsqueeze(1).broadcast_to([128, PT, 16]), ALU.add))
            vec(lambda e: e.tensor_tensor(zidx, base, cnt, ALU.add))
            vec(lambda e: e.scalar_tensor_tensor(out=zidx, in0=zidx, scalar=iotas, in1=spare, op0=ALU.add, op1=ALU.subtract))
            vec(lambda e: e.scalar_tensor_tensor(out=zpad, in0=ntile, scalar=128.0, in1=cnt, op0=ALU.mult, op1=ALU.subtract))
            vec(lambda e: e.tensor_scalar(zpad, zpad, iotas, None, ALU.is_gt))
            vec(lambda e: e.tensor_tensor(zidx, zidx, zpad, ALU.mult))
            vec(lambda e: e.tensor_tensor(R["zidu"][:, p, :], zidx, spare, ALU.add))
            ready["zi", p] = last[0]
            yield
            sidx = other.rearrange("p t e -> p (t e)")[:, 0:4 * PT].rearrange("p (t j) -> p t j", j=4)
            for j in range(TOPK):
                for src, dst in ((slot, sidx[:, :, j]), (cm, wts[:, T0:T0 + PT, j])):
                    vec(lambda e, src=src, j=j: e.scalar_tensor_tensor(
                        out=inc, in0=rk, scalar=float(j), in1=src, op0=ALU.is_equal, op1=ALU.mult))
                    vec(lambda e, dst=dst: e.tensor_reduce(dst, inc, AX.X, ALU.add))
                yield
            vec(lambda e: e.tensor_copy(sidu[:, T0:T0 + PT, :], sidx))
            ready["idx", p] = last[0]
            vec(lambda e: e.memset(tie, 0.0))
            for z in range(E):
                vec(lambda e, z=z: e.tensor_scalar(tic, tix, ce_[0:1, z:z + 1], None, ALU.is_ge))
                vec(lambda e: e.tensor_tensor(tie, tie, tic, ALU.add))
                if z % 3 == 2:
                    yield
            vec(lambda e: e.tensor_copy(tile_e[p][:, :], tie))
            ready["rt", p] = last[0]
            yield

        def scatter(p):
            ends = {}
            rows = {}

            def fetch(t_):
                i, k = FIRST[p] + t_, (hs_n[0] + t_) % 3
                rows[t_] = load(R["hs"][:, k], h2_d[128 * i:128 * i + 128, :], f"l_hs{k}", [h2_tok[i], hs_free[k], ready["idx", 0]])

            fetch(0)
            fetch(1)
            for z in range(E):
                ready["z", p] = Q.add("gpsimd", lambda e, z=z: e.indirect_dma_start(
                    xg_d[p][:, :], bass.IndirectOffsetOnAxis(R["zidu"][:, p, z:z + 1], 0), R["zr"][:, :], None),
                    after=[ready["zi", p], t_tail[p], ready["zr"]], mark=f"w_z{p}", dma=True)
            for t_ in range(TILES[p]):
                i, k = FIRST[p] + t_, (hs_n[0] + t_) % 3
                for j in range(TOPK):
                    ends[k] = hs_free[k] = Q.add("gpsimd", lambda e, i=i, j=j, k=k: e.indirect_dma_start(
                        xg_d[p][:, :], bass.IndirectOffsetOnAxis(sidu[:, i, j:j + 1], 0), R["hs"][:, k], None),
                        after=[ready["idx", p], ready["z", p], rows[t_]], mark=f"w_s{p}{k}", dma=True)
                if t_ + 2 < TILES[p]:
                    fetch(t_ + 2)
                yield
            hs_n[0] += TILES[p]
            ready["slots", p] = tuple(ends.values())

        def chain(*gens):
            for f in gens:
                yield from f

        def drain(f):
            for _ in f:
                pass

        for g in range(16):
            pump = []
            if g % 4 == 0 and g > 0:
                pump.append((project(g // 4 - 1), 6))
            if g == 15:
                pump.append((route(0), 2))
            group(g, pump)
            for f, _ in pump:
                drain(f)
        for x_ in pend:
            t_end = pv(*x_)
            tick()
        while late:
            tick()

        top = A.at
        A.at = ffn_at
        W13 = A("W13", [128, 2, NE, 2 * I], F32)
        W2 = A("W2", [128, NE, 2, 256], F32)
        xT = A("xT", [128, 2, 2, 128], F32)
        sl = A("sl", [128, 2, I], F32)
        ha = A("ha", [128, 2, I], F32)
        haT = A("haT", [128, 2, 2, 128], F32)
        yo = A("yo", [128, 2, 256], F32)
        xs = A("xs", [128, 2, 256], F32)
        xq = A("xq", [128, 3, 256], F32)
        A.at = on_at
        GB = A("GB", [128, 4, 256], F32)
        yg = A("yg", [128, 2, 4, 256], F32)
        yc = A("yc", [128, 2, 256], F32)
        x2 = A("x2", [128, 2, 256], F32)
        assert A.at <= route_at

        unit_banks[:] = [7]
        bank7[0] = o_free[0]
        t_ew = {}
        for n, lo, hi in ((E, E, NE), (0, 0, 4), (4, 4, 8), (8, 8, 12), (12, 12, E)):
            for f in (0, 1):
                load(W13[:, f, lo:hi], w13[f, :, lo:hi], f"l_ew{n}", [t_end])
            load(W2[:, lo:hi, 0, :], w2[0:128, lo:hi], f"l_ew{n}", [t_end])
            t_ew[n] = load(W2[0:64, lo:hi, 1, :], w2[128:192, lo:hi], f"l_ew{n}", [t_end])

        xT_free = [t_end, t_end]
        xq_free = [t_end] * 3
        xT_psum = [st_read[0], st_read[0]]
        gu_free = [st_read[1]] * 2
        sl_free = [None] * 2
        ha_free = [None] * 2
        ht_free = [tuple(unit_read[-3:])] * 2
        haT_free = [t_end] * 2
        y_free = [tuple(unit_read[-3:])]
        yo_free = [None] * 2
        xs_free = [t_end] * 2
        written = {}
        regs = {}

        def job_load(n, job):
            kind, p, i = job
            src, after = (xg_d[p], [ready["slots", p]]) if kind == "x" else (h2_d, [h2_tok[i]])
            return load(xq[:, n % 3], src[128 * i:128 * i + 128, :], f"l_q{n % 3}", [*after, xq_free[n % 3]])

        def job_in(n, job, tl):
            k = n % 2
            for f in (0, 1):
                t = Q.add("tensor", lambda e, f=f: e.transpose(PB[:, k, 128 * f:128 * f + 128], xq[:, n % 3, 128 * f:128 * f + 128], ident[:, :]),
                          after=[tl, xT_psum[k]], mark="jt")
            xq_free[n % 3] = t
            t = Q.add("scalar", lambda e: e.activation(xT[:, k], PB[:, k, 0:256].rearrange("p (f q) -> p f q", f=2), ACT.Copy),
                      after=[t, xT_free[k]], mark="xT")
            xT_psum[k] = t
            return t

        RB = 8

        def expert_of(job, eng):
            kind, p, i = job
            if kind != "x":
                return None
            if (p, i) not in regs:
                n = min(RB, NI[p] + 1 - i)
                half = i // RB % 2 * RB
                eng.load(pe_regs[half:half + n], tile_e[p][0:1, i:i + n])
                for j in range(n):
                    regs[p, i + j] = eng.snap(pe_regs[half + j], min_val=0, max_val=E)
            return regs[p, i]

        pe_regs = []

        def job_gate(n, job, tx):
            kind, p, i = job
            k = n % 2
            need = [ready["rt", p], *t_ew.values()] if kind == "x" else [t_ew[E]]
            for f in (0, 1):
                def mm(e, f=f):
                    ex = expert_of(job, e)
                    w = W13[:, f, E, :] if ex is None else W13[:, f, bass.ds(ex, 1), :]
                    return e.matmul(PB[:, 2 + k, 0:2 * I], xT[:, k, f, :], w, start=f == 0, stop=f == 1)
                t = Q.add("tensor", mm, after=[tx, gu_free[k], *need], mark="gu")
            xT_free[k] = t
            ts = Q.add("scalar", lambda e: e.activation(sl[:, k], PB[:, 2 + k, 0:I], ACT.Silu), after=[t, sl_free[k]], mark="sl")
            t = Q.add("vector", lambda e: e.tensor_tensor(ha[:, k], sl[:, k], PB[:, 2 + k, I:2 * I], ALU.mult),
                      after=[ts, ha_free[k]], mark="ha")
            gu_free[k] = sl_free[k] = t
            return t

        def job_turn(n, job, th):
            k = n % 2
            Q.add("tensor", lambda e: e.transpose(PB[:, 4 + k, 0:128], ha[:, k, 0:128], ident[:, :]), after=[th, ht_free[k]], mark="ht")
            t = Q.add("tensor", lambda e: e.transpose(PB[0:64, 4 + k, 128:256], ha[:, k, 128:192], ident[:, :]), mark="ht")
            ha_free[k] = t
            Q.add("scalar", lambda e: e.activation(haT[:, k, 0, :], PB[:, 4 + k, 0:128], ACT.Copy), after=[t, haT_free[k]], mark="haT")
            t = Q.add("scalar", lambda e: e.activation(haT[0:64, k, 1, :], PB[0:64, 4 + k, 128:256], ACT.Copy), mark="haT")
            ht_free[k] = t
            return t

        def job_down(n, job, ta, tl):
            kind, p, i = job
            k = n % 2

            def mm(e, half):
                ex = expert_of(job, e)
                rows = slice(0, 128) if half == 0 else slice(0, 64)
                w = W2[rows, E, half, :] if ex is None else W2[rows, bass.ds(ex, 1), half, :]
                return e.matmul(PB[:, 6, 0:256], haT[rows, k, half, :], w, start=half == 0, stop=half == 1)
            Q.add("tensor", lambda e: mm(e, 0), after=[ta, y_free[0]], mark="dn")
            t = Q.add("tensor", lambda e: mm(e, 1), mark="dn")
            haT_free[k] = t
            if kind == "x":
                t = Q.add("vector", lambda e: e.tensor_copy(yo[:, k], PB[:, 6, 0:256]), after=[t, yo_free[k]], mark="yo")
                y_free[0] = t
                yo_free[k] = Q.add("sync", lambda e: e.dma_start(y_d[p][128 * i:128 * i + 128, :], yo[:, k]), after=[t],
                                   mark=f"w_y{p}{k}", dma=True)
                written["y", p, k] = yo_free[k]
            else:
                t = Q.add("vector", lambda e: e.tensor_copy(yo[:, k], PB[:, 6, 0:256]), after=[t, yo_free[k]], mark="yo")
                y_free[0] = t
                yo_free[k] = Q.add("sync", lambda e: e.dma_start(x2_d[128 * i:128 * i + 128, :], yo[:, k]), after=[t],
                                   mark=f"w_x2{p}{k}", dma=True)
                written["x2", p, k] = yo_free[k]

        yg_free = [None] * 2
        yc_free = [None] * 2
        x2_free = [None] * 2
        xs_free = [t_end] * 2

        def combine(p):
            wy = [written["y", p, k] for k in (0, 1)]
            end = [proj_tok[3, t_] for t_ in range(16)] + [l_tok[NT - 1]]
            if p == 0:
                now["gb"] = load(GB[:, :, :], mod_d[1].partition_broadcast(128), "l_gb", end)
            rows = {}

            def fetch(t_):
                i, k = FIRST[p] + t_, t_ % 2
                load(xs[:, k], x1_d[128 * i:128 * i + 128, :], f"l_x2{k}", [x1_tok[i], xs_free[k]])
                t = load(x2[:, k], x2_d[128 * i:128 * i + 128, :], f"l_x2{k}", [*end, x2_free[k], written["x2", p, 0], written["x2", p, 1]])
                for j in range(TOPK):
                    tg = Q.add("gpsimd", lambda e, j=j: e.indirect_dma_start(
                        yg[:, k, j, :], None, y_d[p][:, :], bass.IndirectOffsetOnAxis(sidu[:, i, j:j + 1], 0)),
                        after=[*wy, *end, yg_free[k]], mark=f"l_yg{k}", dma=True)
                rows[t_] = (t, tg)

            fetch(0)
            yield
            for t_ in range(TILES[p]):
                i, k = FIRST[p] + t_, t_ % 2
                if t_ + 1 < TILES[p]:
                    fetch(t_ + 1)
                yield
                tx2, tg = rows[t_]
                t = Q.add("vector", lambda e, i=i, k=k: e.scalar_tensor_tensor(
                    out=yc[:, k], in0=yg[:, k, 0, :], scalar=wts[:, i, 0:1], in1=x2[:, k], op0=ALU.mult, op1=ALU.add),
                    after=[tg, tx2, yc_free[k], ready["rt", p]], mark="cb")
                x2_free[k] = t
                for j in range(1, TOPK):
                    t = Q.add("vector", lambda e, i=i, k=k, j=j: e.scalar_tensor_tensor(
                        out=yc[:, k], in0=yg[:, k, j, :], scalar=wts[:, i, j:j + 1], in1=yc[:, k], op0=ALU.mult, op1=ALU.add),
                        after=[t], mark="cb")
                yg_free[k] = t
                t = Q.add("vector", lambda e, k=k, i=i: e.tensor_tensor(yc[:, k], yc[:, k], GB[:, i // 16], ALU.mult), after=[t, now["gb"]], mark="cb")
                t = Q.add("vector", lambda e, k=k: e.tensor_tensor(yc[:, k], yc[:, k], xs[:, k], ALU.add), after=[t], mark="cb")
                xs_free[k] = t
                yc_free[k] = Q.add("sync", lambda e, i=i, k=k: e.dma_start(out[128 * i:128 * i + 128, :], yc[:, k]),
                                   after=[t], mark=f"w_o{k}", dma=True)
                yield

        lag = []
        count = [0]

        def run(jobs, *pumps):
            pumps = [[f, 0.0, rate] for f, rate in pumps]
            n0 = count[0]
            rows = {}

            def ahead(m):
                if m < len(jobs):
                    rows[m] = job_load(n0 + m, jobs[m])

            ahead(0)
            ahead(1)
            for m, job in enumerate([*jobs, None, None, None]):
                if job is not None:
                    n = count[0]
                    count[0] += 1
                    lag.append([n, job, 0, None, rows.get(m)])
                for x_ in list(lag):
                    n, jb, st_, tk, tl = x_
                    if st_ == 0:
                        x_[3] = job_in(n, jb, tl)
                        ahead(m + 2)
                    elif st_ == 1:
                        x_[3] = job_gate(n, jb, tk)
                    elif st_ == 2:
                        x_[3] = job_turn(n, jb, tk)
                    else:
                        job_down(n, jb, tk, tl)
                        lag.remove(x_)
                    x_[2] += 1
                for f in pumps:
                    f[1] += f[2]
                    while f[1] >= 1:
                        f[1] -= 1
                        next(f[0], None)
            for f in pumps:
                drain(f[0])

        routed = [[("x", p, i) for i in range(NI[p])] for p in range(PARTS)]
        run([("s", 0, i) for i in range(FIRST[1])], (chain(project(3), route(1)), 4), (scatter(0), 0.75))
        run([("s", 1, i) for i in range(FIRST[1], NT)], (scatter(1), 0.5))
        run(routed[0])
        run(routed[1], (combine(0), 1.8))
        drain(combine(1))
        Q.pause("sync", [(k, v) for k, v in Q.everything() if k.startswith("w_")])

        block = ctx.enter_context(nc.Block())

        @block.sync
        def _(eng):
            Q.play("sync", eng)

        @block.tensor
        def _(eng):
            pe_regs.extend(eng.alloc_register(f"expert{j}") for j in range(2 * RB))
            Q.play("tensor", eng)

        @block.vector
        def _(eng):
            Q.play("vector", eng)

        @block.scalar
        def _(eng):
            Q.play("scalar", eng)

        @block.gpsimd
        def _(eng):
            Q.play("gpsimd", eng)


def tables():
    inv = (1.0 / (np.float32(10000.0) ** (np.arange(0, HD, 2, dtype=np.float32) / np.float32(HD)))).astype(np.float32)
    fr = np.arange(T, dtype=np.float32)[:, None] * inv[None, :]
    rope = np.concatenate([np.sin(fr.astype(np.float64)), np.cos(fr.astype(np.float64))], -1).astype(np.float32)
    s, c = rope[:, 0::2].T, rope[:, 1::2].T
    k = np.arange(128)
    cons = np.zeros((128, 2, 128), np.float32)
    cons[:, 0, :] = np.eye(128, dtype=np.float32)
    cons[:, 1, :] = np.where(k[None, :] > k[:, None], np.float32(-BIG), np.float32(0))
    n = NI[0] + 1
    fcon = np.zeros((128, 48 + n + 1 + 2 * E), np.float32)
    fcon[:, 0:48] = 128 * np.arange(48)
    fcon[:, 48:48 + n] = np.arange(n)
    fcon[:, 48 + n] = k
    for p in range(PARTS):
        fcon[:, 49 + n + E * p:49 + n + E * p + E] = (NI[p] + 1 + np.arange(E)[None, :]) * 128 + k[:, None]
    return np.ascontiguousarray(np.tile(c, (16, 1))), np.ascontiguousarray(np.tile(s, (16, 1))), cons, fcon


def kernel(L0_attn_x, L0_attn_qkv_w, L0_attn_qkv_b, L0_attn_out_w, L0_attn_out_b, L0_ffn_gate_w, L0_ffn_gate_bias,
           L0_ffn_w1, L0_ffn_w2, L0_ffn_w3, L0_ffn_ws1, L0_ffn_ws2, L0_ffn_ws3, L0_c, L0_wmod):
    import concourse.bacc as bacc
    from concourse.bass_utils import run_bass_kernel_spmd

    a = np.ascontiguousarray
    qkv_w, qkv_b = np.asarray(L0_attn_qkv_w), np.asarray(L0_attn_qkv_b)
    head = np.arange(H)[:, None] * HD
    cols = [(z * D + head + 2 * np.arange(8)[None, :] + o).reshape(-1) for z in (0, 1) for o in (0, 1)]
    wo = np.zeros((4, 4, 32, D), np.float32)
    wo[:, :, 0:HD, :] = np.asarray(L0_attn_out_w).reshape(4, 4, HD, D)
    w1 = np.concatenate([np.asarray(L0_ffn_w1), np.asarray(L0_ffn_ws1)[None]], 0)
    w3 = np.concatenate([np.asarray(L0_ffn_w3), np.asarray(L0_ffn_ws3)[None]], 0)
    w2 = np.concatenate([np.asarray(L0_ffn_w2), np.asarray(L0_ffn_ws2)[None]], 0)
    w13 = np.concatenate([w1, w3], 1).transpose(2, 0, 1).reshape(2, 128, NE, 2 * I)
    ropec, ropes, cons, fcon = tables()
    arrays = {
        "x": a(np.asarray(L0_attn_x).reshape(N, D)),
        "wqk": a(qkv_w[:, np.concatenate(cols)]),
        "wv": a(qkv_w[:, 2 * D:]),
        "bqk": a(np.stack([qkv_b[c] for c in cols], 1)),
        "bv": a(qkv_b[2 * D:]),
        "wo": a(wo.reshape(4, 128, D).transpose(1, 0, 2)),
        "ob": a(np.asarray(L0_attn_out_b)),
        "gw": a(np.asarray(L0_ffn_gate_w).T),
        "gbias": a(np.asarray(L0_ffn_gate_bias)),
        "w13": a(w13),
        "w2": a(w2.transpose(2, 0, 1)),
        "cT": a(np.asarray(L0_c).T.reshape(2, 128, B).transpose(1, 0, 2)),
        "wmod": a(np.asarray(L0_wmod)),
        "ropec": ropec,
        "ropes": ropes,
        "consts": cons,
        "fconst": fcon,
    }
    nc = bacc.Bacc("TRN2", target_bir_lowering=False, num_devices=1)
    args = {n: nc.dram_tensor(f"in_{n}", v.shape, mybir.dt.from_np(v.dtype), kind="ExternalInput").ap()
            for n, v in arrays.items()}
    args["out"] = nc.dram_tensor("out_0", (N, D), F32, kind="ExternalOutput").ap()
    program(nc, **args)
    got = run_bass_kernel_spmd(nc, [{f"in_{n}": v for n, v in arrays.items()}], core_ids=[0])
    return got.results[0]["out_0"].reshape(B, T, D)
```

```python
from contextlib import ExitStack

import numpy as np

import concourse.bass as bass
from concourse import mybir

F32 = mybir.dt.float32
I32 = mybir.dt.int32
U32 = mybir.dt.uint32
BF16 = mybir.dt.bfloat16
ALU = mybir.AluOpType
ACT = mybir.ActivationFunctionType
AX = mybir.AxisListType

B, T, D, H, HD = 4, 2048, 256, 16, 16
N = B * T
NT = N // 128
E, I, G = 16, 192, 4
NE = E + 1
TOPK = 4
PARTS = 2
FIRST = (0, 32)
TILES = (32, 32)
MT = max(TILES)
NI = tuple(n * TOPK + E - 1 for n in TILES)
BIG = 1e30
EPS = 1e-5


class Queues:

    ENGINES = ("sync", "tensor", "vector", "scalar", "gpsimd")

    def __init__(self, nc, ctx):
        self.nc, self.ctx = nc, ctx
        self.q = {e: [] for e in self.ENGINES}
        self.sem, self.count = {}, {}

    def add(self, engine, fn, after=(), mark=None, dma=False):
        if mark is not None:
            if mark not in self.sem:
                self.sem[mark] = self.ctx.enter_context(self.nc.semaphore(mark))
                self.count[mark] = 0
            self.count[mark] += 16 if dma else 1
        flat = [x for t in after if t is not None for x in ([t] if isinstance(t[0], str) else t)]
        self.q[engine].append((fn, tuple(flat), mark, 16 if dma else 1))
        return None if mark is None else (mark, self.count[mark])

    def everything(self):
        return list(self.count.items())

    def pause(self, engine, tokens):
        self.q[engine].append((None, tuple(tokens), None, 0))

    def play(self, engine, eng):
        seen = {}
        for fn, after, mark, inc in self.q[engine]:
            for name, value in after:
                if seen.get(name, 0) < value:
                    eng.wait_ge(self.sem[name], value)
                    seen[name] = value
            if fn is None:
                continue
            ins = fn(eng)
            if mark is not None:
                ins.then_inc(self.sem[mark], inc)


class Arena:

    def __init__(self, nc, at, end=None):
        self.nc, self.at, self.end = nc, at, end

    def __call__(self, name, shape, dt):
        size = (int(np.prod(shape[1:])) * (2 if dt == BF16 else 4) + 31) // 32 * 32
        assert self.end is None or self.at + size <= self.end, name
        t = self.nc.alloc_sbuf_tensor_at(name, shape, dt, offset=self.at)
        self.at += size
        return t


def program(nc, x, wqk, wv, bqk, bv, wo, ob, gw, gbias, w13, w2, cT, wmod, ropec, ropes, consts, fconst, out):
    def scratch(name, shape, dt=F32):
        return nc.dram_tensor(name, shape, dt, kind="Internal").ap()

    parts_d = scratch("qk_parts", [B, H, 2, 3, HD, T], BF16)
    v_d = scratch("v_rows", [B, 4, 128, T // 128, 68])
    x1_d = scratch("x1_rows", [N, D])
    h2_d = scratch("h2_rows", [N, D])
    x2_d = scratch("x2_rows", [N, D])
    mod_d = scratch("mod_rows", [4, B, D])
    rd_d = scratch("rden_rows", [64, 4, 512])
    xg_d = [scratch(f"x_slots{p}", [(NI[p] + 1 + E) * 128, D]) for p in range(PARTS)]
    y_d = [scratch(f"y_slots{p}", [NI[p] * 128, D]) for p in range(PARTS)]

    with ExitStack() as ctx:
        Q = Queues(nc, ctx)
        PB = ctx.enter_context(nc.psum_tensor("PB", [128, 8, 512], F32))
        A = Arena(nc, (int(nc.sbuf_base) + 31) // 32 * 32)

        ident = A("ident", [128, 128], F32)
        identb = A("identb", [128, 128], BF16)
        m1 = A("m1", [128, 128], BF16)
        mhalf = A("mhalf", [128, 4], F32)
        mT = A("mT", [128, 4, 4], F32)
        obB = A("obB", [128, 256], F32)
        wo_s = A("wo_s", [128, 4, 256], F32)

        mx = A("mx", [128, 4, 16, 4], F32)
        nm = A("nm", [128, 4, 16], F32)
        nh = A("nh", [16, 2, 2, 128], BF16)
        nh_end = A.at
        L = A("L", [128, NT, 16], F32)
        sidu = A("sidu", [128, NT, 4], U32)
        wts = A("wts", [128, NT, 4], F32)
        tile_e = [A(f"tile_e{p}", [1, NI[p] + 1], I32) for p in range(PARTS)]
        gw_s = A("gw_s", [128, 2, 16], F32)
        gbB = A("gbB", [128, 16], F32)
        FC = MT + NI[0] + 1 + 1 + 2 * E
        fc_s = A("fc_s", [128, FC], F32)
        osb = A("osb", [128, 2, 512], F32)
        d16 = A("d16", [128, 2, 16], F32)
        r16 = A("r16", [128, 2, 16], F32)
        rden = A("rden", [128, 2, 512], F32)
        XI = 5
        xin = A("xin", [128, XI, 256], F32)
        xo = A("xo", [128, 2, 256], F32)
        h2t = A("h2t", [128, 3, 256], F32)
        lT = A("lT", [128, 2, 128], F32)
        gaB = A("gaB", [128, 256], F32)
        modB = A("modB", [128, 2, 256], F32)
        st6f = A("st6f", [128, 2, 6], F32)
        mvf = A("mvf", [128, 2, 2], F32)
        vef = A("vef", [128, 2], F32)
        rsf = A("rsf", [128, 2], F32)
        R = {n: A(n, [128, MT, 16], F32) for n in ("sg", "sb_", "rk", "cm", "sa")}
        R["selb"] = A("selb", [128, MT, 16], BF16)
        R["wsum"] = A("wsum", [128, MT], F32)
        R.update({n: A(n, [128, 16], F32) for n in ("cnt", "ntile", "zidx", "zpad")})
        R["cend"] = A("cend", [128, 2, 16], F32)
        R["zidu"] = A("zidu", [128, PARTS, 16], U32)
        R["utri"] = A("utri", [128, 128], BF16)
        R["onesb"] = A("onesb", [128, 128], BF16)
        on_at = A.at
        ON = A("ON", [128, 4, T], F32)
        qo_at = A.at
        QO = A("QO", [98, 3, 4, T], BF16)
        ko_at = A.at
        KO = A("KO", [98, 3, 4, T], BF16)
        v_at = A.at
        V = A("V", [128, 2, 16, 68], F32)
        NP = 5
        P = A("P", [128, NP, 2, 512], F32)
        assert A.at <= int(nc.sbuf_usable_end)

        def load(dst, src, mark, after=()):
            return Q.add("sync", lambda e: e.dma_start(dst, src), after=after, mark=mark, dma=True)

        now = {}
        def load_g(g, after):
            b, h0, s = g // 4, 4 * (g % 4), (g + 2) % 3
            for dst, z, plan in ((QO, 0, ((0, 0, 3), (48, 0, 2), (80, 0, 1))),
                                 (KO, 1, ((0, 0, 1), (16, 0, 1), (32, 0, 1), (48, 1, 1), (64, 1, 1), (80, 2, 1)))):
                for row, k, n in plan:
                    t = load(dst[row:row + 16 * n, s], parts_d[b, h0:h0 + 4, z, k:k + n].rearrange("h k d t -> (k d) h t"), f"l_g{s}", after)
            return t

        def load_v(g, after):
            return load(V[:, g % 2], v_d[g // 4, g % 4], f"l_v{g % 2}", after)

        units = [0]
        unit_read = []
        unit_banks = [1, 7]
        bank7 = [None]

        def unit_bank():
            u = units[0]
            units[0] += 1
            if len(unit_banks) == 1:
                return 7, bank7[0] if bank7[0] is not None else unit_read[u - 1]
            n = len(unit_banks)
            return unit_banks[u % n], unit_read[u - n] if u >= n else None

        def unit_done(t):
            unit_read.append(t)
            if len(unit_banks) == 1:
                bank7[0] = None

        nm_dma = {}
        loaded = {}
        loaded_v = {}

        def max_units(g):
            s = (g + 2) % 3
            for j in range(4):
                for t in range(16):
                    n_all = 128 * (t + 1)
                    for kc in range((n_all + 511) // 512):
                        def emit(j=j, t=t, kc=kc, n=min(512, n_all - 512 * kc), last=512 * kc + 512 >= n_all):
                            bank, free = unit_bank()
                            tk = Q.add("tensor", lambda e: e.matmul(
                                PB[:, bank, 0:n], QO[0:96, s, j, 128 * t:128 * t + 128],
                                KO[0:96, s, j, 512 * kc:512 * kc + n], start=True, stop=True),
                                after=[loaded[g], free], mark="s")
                            if last:
                                tk = Q.add("tensor", lambda e: e.matmul(
                                    PB[:, bank, n - 128:n], identb[:, :], m1[:, :], start=False, stop=True,
                                    skip_group_check=True), mark="s")
                            now["mx"] = Q.add("vector", lambda e: e.tensor_reduce(
                                mx[:, j, t, kc:kc + 1], PB[:, bank, 0:n], AX.X, ALU.max), after=[tk], mark="mx")
                            unit_done(now["mx"])
                        yield emit

                def fin(j=j):
                    now["nm"] = Q.add("vector", lambda e: e.tensor_reduce(nm[:, j, :], mx[:, j], AX.X, ALU.max, negate=True),
                                      after=[now["mx"]], mark="nm")
                yield fin

                def turn(j=j):
                    bank, free = unit_bank()
                    tk = Q.add("tensor", lambda e: e.transpose(PB[0:16, bank, 0:128], nm[:, j, :], ident[:, :]),
                               after=[now["nm"], free], mark="s")
                    tk = Q.add("vector", lambda e: e.tensor_copy(nh[:, j % 2, 0, :], PB[0:16, bank, 0:128]),
                               after=[tk, nm_dma.get((g, j - 2) if j > 1 else (g - 1, j + 2))], mark="nh")
                    tk = Q.add("vector", lambda e: e.tensor_tensor(nh[:, j % 2, 1, :], PB[0:16, bank, 0:128], nh[:, j % 2, 0, :],
                                                                   ALU.subtract), after=[tk], mark="mx")
                    unit_done(tk)
                    for k in (0, 1):
                        nm_dma[g, j] = Q.add("gpsimd", lambda e, k=k: e.dma_start(
                            QO[96 + k:97 + k, s, j, :].rearrange("o (t q) -> o t q", q=128),
                            nh[:, j % 2, k, :]), after=[tk, loaded[g]], mark=f"w_nm{j}", dma=True)
                yield turn

        set2 = 2 * 4 * T * 2
        pools = [Arena(nc, nh_end, qo_at), Arena(nc, v_at + 16 * 68 * 4, int(nc.sbuf_usable_end))]
        late_pools = [Arena(nc, qo_at, qo_at + set2), Arena(nc, ko_at, ko_at + set2)]

        def A_(name, shape, dt, pools=pools):
            size = (int(np.prod(shape[1:])) * (2 if dt == BF16 else 4) + 31) // 32 * 32
            pool = next(p for p in [*pools, *late_pools] if p.at + size <= p.end)
            return pool(name, shape, dt)

        XT, PT_ = 3, 3
        pt = [A_(f"pt{w}", [128, 3, 4, 512], BF16, late_pools) for w in range(PT_)]
        vst = A_("vst", [128, 2, 4, 4, 68], F32, late_pools)
        wm_s = A_("wm_s", [128, 2, 1536], F32)
        cT_s = A_("cT_s", [128, 2, 4], F32)
        ce = A_("ce", [128, 2, 4], F32)
        cd = A_("cd", [128, 2, 4], F32)
        cr = A_("cr", [128, 2, 4], F32)
        sc = A_("sc", [128, 2, 4], F32)
        cons = A_("cons", [128, 2, 128], F32)
        graw = A_("graw", [4, 4, 256], F32)
        gneg = A_("gneg", [4, 2, 256], F32)
        gsg = A_("gsg", [4, 2, 256], F32)
        wqk_s = A_("wqk_s", [128, 2, 512], F32)
        wv_s = A_("wv_s", [128, 2, 256], F32)
        bqk_s = A_("bqk_s", [128, 4], F32)
        bv_s = A_("bv_s", [128, 4], F32)
        bvB = A_("bvB", [128, 4, 128], F32)
        r = A_("r", [128, 2, 4, 512], F32)
        pe_ = A_("pe_", [128, 2, 4, 512], F32)
        rC = A_("rC", [128, T], F32)
        rS = A_("rS", [128, T], F32)
        xt = A_("xt", [128, XT, 4, 256], F32)
        xn = A_("xn", [128, 2, 4, 256], F32)
        hT = A_("hT", [128, 2, 2, 512], F32)
        ta = A_("ta", [128, 2, 512], F32)
        tb = A_("tb", [128, 2, 512], F32)
        st6 = A_("st6", [128, 2, 4, 6], F32)
        mv = A_("mv", [128, 2, 4, 2], F32)
        ve = A_("ve", [128, 2, 4], F32)
        rstd = A_("rstd", [128, 2, 4], F32)

        xch = x.rearrange("(c t p) d -> c p t d", t=4, p=128)
        x_free = [None] * XT
        tx = {}

        def load_x(c):
            tx[c] = load(xt[:, c % XT], xch[c], f"l_x{c % XT}", [x_free[c % XT]])

        load(cT_s[:, :, :], cT, "l_mod")
        t_cons = load(cons[:, :, :], consts, "l_mod")
        load_x(0)
        t_wm = load(wm_s[:, :, :], wmod.rearrange("(k p) n -> p k n", p=128), "l_wm")
        load_x(1)
        load(wqk_s[:, :, :], wqk.rearrange("(k p) n -> p k n", p=128), "l_w")
        load(wv_s[:, :, :], wv.rearrange("(k p) n -> p k n", p=128), "l_w")
        load(bqk_s[:, :], bqk, "l_w")
        load(rC[:, :], ropec, "l_w")
        t_w = load(rS[:, :], ropes, "l_w")
        load_x(2)
        load(bv_s[:, :], bv, "l_o")
        load(obB[:, :], ob.partition_broadcast(128), "l_o")
        t_o = load(wo_s[:, :, :], wo, "l_o")

        t = Q.add("scalar", lambda e: e.activation(ce[:, :, :], cT_s[:, :, :], ACT.Exp, scale=-1.0),
                  after=[t_cons], mark="c_exp")
        t = Q.add("vector", lambda e: e.tensor_scalar(cd[:, :, :], ce[:, :, :], 1.0, None, ALU.add), after=[t, t_cons], mark="c_v")
        t = Q.add("vector", lambda e: e.reciprocal(cr[:, :, :], cd[:, :, :]), after=[t], mark="c_v")
        t_sc = Q.add("vector", lambda e: e.tensor_tensor(sc[:, :, :], cT_s[:, :, :], cr[:, :, :], ALU.mult), after=[t], mark="c_v")
        Q.add("vector", lambda e: e.tensor_copy(ident[:, :], cons[:, 0, :]), mark="c_k")
        Q.add("vector", lambda e: e.tensor_copy(identb[:, :], cons[:, 0, :]), mark="c_k")
        Q.add("vector", lambda e: e.tensor_copy(m1[:, :], cons[:, 1, :]), mark="c_k")
        t_mx = Q.add("vector", lambda e: e.memset(mx[:, :, :, :], -3.0e38), mark="c_k")
        t_k = Q.add("vector", lambda e: e.memset(mhalf[:, :], -0.5), mark="c_k")
        Q.pause("vector", [t_mx])
        t_vst = Q.add("gpsimd", lambda e: e.memset(vst[:, :, :, :, :], 1.0), mark="c_p")
        t_ones = [None, None]
        t_ones[0] = Q.add("gpsimd", lambda e: e.memset(KO[96:98, 2, :, :], 1.0), after=[t_vst], mark="c_p")
        Q.pause("gpsimd", [t_ones[0]])

        def p_mod():
            for n, (kind, f) in enumerate([(k, f) for k in (0, 1) for f in (0, 1)]):
                for k in (0, 1):
                    col = kind * 256 + f * 128
                    t = Q.add("tensor", lambda e, n=n, k=k, col=col: e.matmul(
                        PB[:, 7, 4 * n:4 * n + 4], wm_s[:, k, col:col + 128], sc[:, k, :], start=k == 0, stop=k == 1),
                        after=[t_wm, t_sc], mark="m_mod")
            t = Q.add("vector", lambda e: e.tensor_copy(mT[:, :, :], PB[:, 7, 0:16].rearrange("p (n b) -> p n b", b=4)),
                      after=[t], mark="c_m")
            return Q.add("vector", lambda e: e.tensor_scalar(mT[:, 2:4, :], mT[:, 2:4, :], 1.0, None, ALU.add), after=[t], mark="c_m")

        def p_gates():
            for n, kind in enumerate((2, 5, 3, 4)):
                for k in (0, 1):
                    t = Q.add("tensor", lambda e, k=k, kind=kind, n=n: e.matmul(
                        PB[0:4, 1 + 5 * (n // 2), 256 * (n % 2):256 * (n % 2) + 256], sc[:, k, :],
                        wm_s[:, k, kind * 256:kind * 256 + 256], start=k == 0, stop=k == 1), mark="m_gate")
            gate, two = graw[:, 0:2, :], PB[0:4, 6, :].rearrange("p (n d) -> p n d", d=256)
            t = Q.add("vector", lambda e: e.tensor_copy(gate, PB[0:4, 1, :].rearrange("p (n d) -> p n d", d=256)), after=[t], mark="c_g")
            Q.add("vector", lambda e: e.tensor_copy(graw[:, 2, :], two[:, 0, :]), mark="c_g")
            Q.add("vector", lambda e: e.tensor_scalar(graw[:, 3, :], two[:, 1, :], 1.0, None, ALU.add), mark="c_g")
            t = Q.add("vector", lambda e: e.tensor_scalar(gneg[:, :, :], gate, -1.0, None, ALU.mult), after=[t], mark="c_g")
            Q.add("vector", lambda e: e.tensor_scalar(gsg[:, :, :], gate, 0.0, 2.0, ALU.is_ge, ALU.mult), mark="c_g")
            t = Q.add("vector", lambda e: e.tensor_tensor(gneg[:, :, :], gate, gneg[:, :, :], ALU.max), after=[t], mark="c_g")
            t = Q.add("vector", lambda e: e.tensor_scalar(gneg[:, :, :], gneg[:, :, :], 0.25, None, ALU.max), after=[t], mark="c_g")
            t = Q.add("vector", lambda e: e.scalar_tensor_tensor(
                out=gate, in0=gsg[:, :, :], scalar=-1.0, in1=gneg[:, :, :], op0=ALU.add, op1=ALU.mult), after=[t], mark="c_g")
            Q.add("sync", lambda e: e.dma_start(mod_d.rearrange("n b d -> b n d"), graw[:, :, :]), after=[t], mark="w_mod", dma=True)
            tb_ = Q.add("gpsimd", lambda e: e.tensor_copy(bvB[:, :, :], bv_s[:, :].unsqueeze(2).broadcast_to([128, 4, 128])),
                        after=[t_o], mark="c_b")
            for gi in range(4):
                to = Q.add("tensor", lambda e, gi=gi: e.matmul(PB[:, 7, 256:512], bvB[:, gi, :], wo_s[:, gi, :],
                                                               start=gi == 0, stop=gi == 3), after=[tb_, t_mT], mark="m_bv")
            to = Q.add("vector", lambda e: e.tensor_tensor(obB[:, :], obB[:, :], PB[:, 7, 256:512], ALU.add), after=[to], mark="c_ob")
            unit_read.extend([t, to])
            units[0] = 2
            v_free[0] = t

        tp_free = [None]
        qk_free = [None] * 4
        v_free = [None]
        hT_free = [None, None]
        r_free = [None, None]
        pe_free = [None, None]
        pt_free = [None] * PT_
        vst_free = [None, None]
        xn_free = [None, None]
        ro = [None, None]

        def p_norm(c):
            s = c % 2
            for i in range(4):
                t = Q.add("vector", lambda e, i=i: e.bn_stats(st6[:, s, i, :], xt[:, c % XT, i, :]), after=[tx[c]], mark="ln")
            for i in range(4):
                t = Q.add("vector", lambda e, i=i: e.bn_aggr(mv[:, s, i, :], st6[:, s, i, :]), after=[t], mark="ln")
            t = Q.add("vector", lambda e: e.tensor_scalar(ve[:, s, :], mv[:, s, :, 1], EPS, None, ALU.add), after=[t], mark="ln")
            now["rs", c] = Q.add("gpsimd", lambda e: e.tensor_tensor(rstd[:, s, :], ve[:, s, :], mhalf[:, :], ALU.pow),
                                 after=[t, t_k], mark="rs")

        def p_rows(c):
            s = c % 2
            for i in range(4):
                t = Q.add("vector", lambda e, i=i: e.tensor_scalar(
                    xn[:, s, i, :], xt[:, c % XT, i, :], mv[:, s, i, 0:1], rstd[:, s, i:i + 1], ALU.subtract, ALU.mult),
                    after=[now["rs", c], xn_free[s]], mark="xn")
            x_free[c % XT] = now["xn", c] = t
            if c + XT < 16:
                load_x(c + XT)

        def p_turn(c, f):
            s, b = c % 2, c // 4
            for i in range(4):
                tt = Q.add("tensor", lambda e, i=i: e.transpose(
                    PB[:, 0, 128 * i:128 * i + 128], xn[:, s, i, 128 * f:128 * f + 128], ident[:, :]),
                    after=[now["xn", c], t_k, tp_free[0]], mark="tp")
            tp_free[0] = now["hT", c] = Q.add("scalar", lambda e: e.activation(
                hT[:, s, f, :], PB[:, 0, :], ACT.Identity, bias=mT[:, f, b:b + 1], scale=mT[:, 2 + f, b:b + 1]),
                after=[tt, t_mT, hT_free[s]], mark="hT")
            xn_free[s] = tt

        def p_qkv(c, between, fill):
            s, b, tok = c % 2, c // 4, (c % 4) * 512
            th = now["hT", c]
            C, S = rC[:, tok:tok + 512], rS[:, tok:tok + 512]

            def rot(dst, bank, tab):
                return lambda e: e.scalar_tensor_tensor(out=dst, in0=PB[:, bank, :], scalar=bqk_s[:, bank - 2:bank - 1],
                                                        in1=tab, op0=ALU.add, op1=ALU.mult)
            for z in (0, 1):
                tq = []
                for m in (2 * z, 2 * z + 1):
                    for f in (0, 1):
                        t = Q.add("tensor", lambda e, m=m, f=f: e.matmul(
                            PB[:, 2 + m, :], wqk_s[:, f, 128 * m:128 * m + 128], hT[:, s, f, :], start=f == 0, stop=f == 1),
                            after=[th, t_w, qk_free[m]], mark="qk")
                        fill()
                    tq.append(t)
                    between(4 * z + m % 2)
                lo, hi = 2 + 2 * z, 3 + 2 * z
                for half, (tl, th_, op) in enumerate(((C, S, ALU.subtract), (S, C, ALU.add))):
                    Q.add("vector", rot(ta[:, half], lo, tl), after=[tq[0], ro[half]], mark="rot")
                    t = Q.add("vector", rot(tb[:, half], hi, th_), after=[tq[1]], mark="rot")
                    ro[half] = Q.add("gpsimd", lambda e, half=half, z=z, op=op: e.tensor_tensor(
                        r[:, s, 2 * z + half, :], ta[:, half], tb[:, half], op), after=[t, r_free[s]], mark="rsum")
                    if half == 0:
                        between(4 * z + 2)
                qk_free[2 * z] = qk_free[2 * z + 1] = t
                for i in (2 * z, 2 * z + 1):
                    for f in (0, 1):
                        t = Q.add("tensor", lambda e, i=i, f=f: e.matmul(
                            PB[:, 6, 256 * (i % 2):256 * (i % 2) + 256], hT[:, s, f, 128 * i:128 * i + 128],
                            wv_s[:, f, :], start=f == 0, stop=f == 1), after=[th, v_free[0]], mark="v")
                    fill()
                for i in (2 * z, 2 * z + 1):
                    v_free[0] = Q.add("scalar", lambda e, i=i: e.activation(
                        vst[:, s, :, i, :].rearrange("p g (h d) -> p g h d", d=17)[:, :, :, 0:16],
                        PB[:, 6, 256 * (i % 2):256 * (i % 2) + 256].rearrange("p (g h d) -> p g h d", g=4, d=16), ACT.Copy),
                        after=[t, vst_free[s], t_vst], mark="vb")
                between(4 * z + 3)
            hT_free[s] = t
            vst_free[s] = Q.add("sync", lambda e: e.dma_start(
                v_d[b].rearrange("g p t e -> p g t e")[:, :, 4 * (c % 4):4 * (c % 4) + 4, :], vst[:, s]),
                after=[v_free[0]], mark=f"w_v{s}", dma=True)
            now["r", c] = ro[1]

        def p_hi(c):
            s, w = c % 2, c % PT_
            t = Q.add("scalar", lambda e: e.activation(pt[w][:, 0], r[:, s], ACT.Copy), after=[now["r", c], pt_free[w]], mark="p_hi")
            r_free[s] = now["rest", c] = Q.add("gpsimd", lambda e: e.tensor_tensor(pe_[:, s], r[:, s], pt[w][:, 0], ALU.subtract),
                                               after=[t, pe_free[s]], mark="p_rest")

        def p_lo(c):
            s, w, b, tok = c % 2, c % PT_, c // 4, (c % 4) * 512
            t = Q.add("scalar", lambda e: e.activation(pt[w][:, 1], pe_[:, s], ACT.Copy), after=[now["rest", c]], mark="p_mid")
            eng = "vector" if c < OWN or c > 13 else "gpsimd"
            t = pe_free[s] = Q.add(eng, lambda e: e.tensor_tensor(pt[w][:, 2], pe_[:, s], pt[w][:, 1], ALU.subtract),
                                   after=[t], mark=f"p_lo_{eng}")
            for z in (0, 1):
                for k in range(3):
                    for half in (0, 1):
                        dst = parts_d[b, :, z, k, 8 * half:8 * half + 8, tok:tok + 512]
                        pt_free[w] = Q.add("sync", lambda e, k=k, z=z, half=half, dst=dst: e.dma_start(
                            dst, pt[w][:, k, 2 * z + half, :]), after=[t], mark=f"w_p{w}", dma=True)

        OWN = 5
        p_norm(0)
        t_mT = p_mod()
        p_rows(0)
        p_turn(0, 0)
        p_norm(1)
        p_turn(0, 1)
        p_gates()
        mu0 = []
        start, hooks, filled = 7, 12 * 9, [0]

        def between(c, k):
            if c + 1 < 16:
                if k == 0:
                    p_rows(c + 1)
                if k == 1:
                    p_turn(c + 1, 0)
                if k == 3 and c + 2 < 16:
                    p_norm(c + 2)
                if k == 3:
                    p_turn(c + 1, 1)
            if k == 0 and c > 0:
                p_hi(c - 1)
            if k == 4 and c > 1:
                p_lo(c - 2)

        def fill(c):
            if c >= start:
                filled[0] += 1
                left = n0 - n0 * filled[0] // hooks
                while len(mu0) > left:
                    mu0.pop(0)()

        for c in range(16):
            p_qkv(c, lambda k, c=c: between(c, k), lambda c=c: fill(c))
            if c == 5:
                loaded[0] = load_g(0, pt_free)
                loaded_v[0] = load_v(0, vst_free)
                mu0.extend(max_units(0))
                n0 = len(mu0)
        p_hi(15)
        p_lo(14)
        p_lo(15)
        while mu0:
            mu0.pop(0)()

        done_p = Q.everything()
        computed = [(k, v) for k, v in done_p if not k.startswith("w_")]

        for e in Q.ENGINES:
            Q.pause(e, done_p if e == "sync" else computed)
        for k in (0, 1):
            t_ones[1] = load(KO[96:98, k, :, :], KO[96:98, 2, :, :], "l_ones")
        t_o0 = Q.add("vector", lambda e: e.memset(PB[:, 7, :], 0.0), mark="a_o0")
        Q.pause("vector", [t_o0])
        unit_banks[:] = [4, 5, 6]

        on_tok = {}
        proj_tok = {}
        xin_free = [None] * XI
        xo_free = [None] * 2
        h2_free = [None] * 3
        lT_free = [None]
        modB_free = [None]
        gaB_free = [None]
        x1_tok, h2_tok, l_tok = {}, {}, {}

        t_rt = load(gw_s[:, :, :], gw.rearrange("(k p) n -> p k n", p=128), "l_rt")
        t_rt = load(fc_s[:, :], fconst, "l_rt")
        t_rt = load(gbB[:, :], gbias.partition_broadcast(128), "l_rt")

        def o_load(b, t):
            i = 16 * b + t
            if t == 0:
                now["ga", b] = load(gaB[:, :], mod_d[0, b].partition_broadcast(128), "l_ga", [gaB_free[0]])
                now["mod", b] = load(modB[:, :, :], mod_d[2:4, b].partition_broadcast(128), "l_mb", [modB_free[0]])
            now["xi", i] = load(xin[:, i % XI], x[128 * i:128 * i + 128, :], f"l_xi{i % XI}", [xin_free[i % XI]])

        def o_proj(b, t):
            i = 16 * b + t
            bank, free = unit_bank()
            for gi in range(4):
                tk = Q.add("tensor", lambda e, gi=gi: e.matmul(
                    PB[:, bank, 0:256], ON[:, gi, 128 * t:128 * t + 128], wo_s[:, gi, :], start=gi == 0, stop=gi == 3),
                    after=[free, on_tok[b, 3, t // 4]], mark="s")
            proj_tok[b, t] = tk
            now["xo", i] = Q.add("vector", lambda e: e.tensor_tensor(xo[:, i % 2], PB[:, bank, 0:256], obB[:, :], ALU.add),
                                 after=[tk, xo_free[i % 2]], mark="xo")
            unit_done(now["xo", i])

        def o_x1(b, t):
            i = 16 * b + t
            tk = Q.add("gpsimd", lambda e: e.tensor_tensor(xo[:, i % 2], xo[:, i % 2], gaB[:, :], ALU.mult),
                       after=[now["xo", i], now["ga", b]], mark="xg")
            gaB_free[0] = tk
            tk = Q.add("gpsimd", lambda e: e.tensor_tensor(xin[:, i % XI], xo[:, i % 2], xin[:, i % XI], ALU.add),
                       after=[tk, now["xi", i]], mark="x1")
            xo_free[i % 2] = now["x1", i] = tk
            x1_tok[i] = Q.add("sync", lambda e: e.dma_start(x1_d[128 * i:128 * i + 128, :], xin[:, i % XI]), after=[tk],
                              mark=f"w_x1{i % XI}", dma=True)

        def o_stat(b, t):
            i = 16 * b + t
            k = i % 2
            tk = Q.add("vector", lambda e: e.bn_stats(st6f[:, k], xin[:, i % XI]), after=[now["x1", i]], mark="ln2")
            tk = Q.add("vector", lambda e: e.bn_aggr(mvf[:, k], st6f[:, k]), after=[tk, now.get(("xn2", i - 2))], mark="ln2")
            tk = Q.add("vector", lambda e: e.tensor_scalar(vef[:, k:k + 1], mvf[:, k, 1:2], EPS, None, ALU.add), after=[tk, now.get(("rs2", i - 2))], mark="ln2")
            now["rs2", i] = Q.add("gpsimd", lambda e: e.tensor_tensor(rsf[:, k:k + 1], vef[:, k:k + 1], mhalf[:, 0:1], ALU.pow),
                                  after=[tk, now.get(("xn2", i - 2))], mark="rs2")

        def o_h2(b, t):
            i = 16 * b + t
            k, k3 = i % 2, i % 3
            tk = Q.add("vector", lambda e: e.tensor_scalar(
                h2t[:, k3], xin[:, i % XI], mvf[:, k, 0:1], rsf[:, k:k + 1], ALU.subtract, ALU.mult),
                after=[now["rs2", i], h2_free[k3]], mark="xn2")
            now["xn2", i] = tk
            xin_free[i % XI] = (tk, x1_tok[i])
            tk = Q.add("gpsimd", lambda e: e.tensor_tensor(h2t[:, k3], h2t[:, k3], modB[:, 1], ALU.mult), after=[tk, now["mod", b]], mark="md2")
            tk = Q.add("gpsimd", lambda e: e.tensor_tensor(h2t[:, k3], h2t[:, k3], modB[:, 0], ALU.add), after=[tk], mark="md2")
            modB_free[0] = now["h2", i] = tk
            h2_tok[i] = Q.add("sync", lambda e: e.dma_start(h2_d[128 * i:128 * i + 128, :], h2t[:, k3]), after=[tk],
                              mark=f"w_h2{k3}", dma=True)

        def o_turn(b, t):
            i = 16 * b + t
            bank, free = unit_bank()
            for f in (0, 1):
                tk = Q.add("tensor", lambda e, f=f: e.transpose(
                    PB[:, bank, 128 * f:128 * f + 128], h2t[:, i % 3, 128 * f:128 * f + 128], ident[:, :]),
                    after=[now["h2", i], free], mark="s")
            h2_free[i % 3] = (tk, h2_tok[i])
            now["lT", i] = Q.add("scalar", lambda e: e.activation(
                lT[:, :, :], PB[:, bank, 0:256].rearrange("p (f q) -> p f q", f=2), ACT.Copy), after=[tk, lT_free[0]], mark="lT")
            unit_done(now["lT", i])

        def o_logits(b, t):
            i = 16 * b + t
            bank, free = unit_bank()
            for f in (0, 1):
                tk = Q.add("tensor", lambda e, f=f: e.matmul(PB[:, bank, 0:16], lT[:, f, :], gw_s[:, f, :],
                                                             start=f == 0, stop=f == 1), after=[now["lT", i], t_rt, free], mark="s")
            lT_free[0] = tk
            l_tok[i] = Q.add("vector", lambda e: e.tensor_copy(L[:, i, :], PB[:, bank, 0:16]), after=[tk], mark="L")
            unit_done(l_tok[i])

        o_stages = (o_load, o_proj, o_x1, o_stat, o_h2, o_turn, o_logits)

        def project(b):
            for it in range(16 + len(o_stages) - 1):
                for d in reversed(range(len(o_stages))):
                    if 0 <= it - d < 16:
                        while o_stages[d] is o_proj and (b, 3, (it - d) // 4) not in on_tok:
                            yield
                        o_stages[d](b, it - d)
                        yield

        st_read = [None, None]
        p_read = [None] * NP
        np_ = [0]
        o_free = [t_o0]
        osb_free = [None, None]
        d16_free = [None, None]
        r16_free = [None, None]
        rd_free = [None, None]
        nchunk = [0]
        done_g = {}
        pend = []
        late = []

        def tick(n=1):
            for _ in range(n):
                for x_ in list(late):
                    x_[0] -= 1
                    if x_[0] <= 0:
                        late.remove(x_)
                        x_[1]()

        def st_one(g, p, c, kt, jj, pb):
            s, j = (g + 2) % 3, 2 * p + jj
            q0 = max(c * 512, kt * 128)
            n = (c + 1) * 512 - q0
            diag = kt >= 4 * c
            tk = Q.add("tensor", lambda e: e.matmul(
                PB[:, j, 0:n], KO[0:98, s, j, 128 * kt:128 * kt + 128], QO[0:98, s, j, q0:q0 + n],
                start=True, stop=True), after=[loaded[g], nm_dma[g, j], t_ones[g > 0], st_read[p]], mark="st")
            if jj == 0:
                return None
            te = st_read[p] = Q.add("scalar", lambda e: e.activation(
                P[:, pb, :, 0:n], PB[:, 2 * p:2 * p + 2, 0:n], ACT.Exp, scale=0.25), after=[tk, p_read[pb]], mark="exp")
            if diag:
                te = Q.add("gpsimd", lambda e: e.affine_select(
                    out=P[:, pb, :, 0:128], in_=P[:, pb, :, 0:128], compare_op=ALU.is_ge, fill=0.0, base=0,
                    pattern=[[0, 2], [1, 128]], channel_multiplier=-1), after=[te], mark="cut")
            return pb, te, q0 - c * 512, n

        def pv(g, c, kt, pair):
            b, gi = g // 4, g % 4
            ch = nchunk[0]
            ob_ = ch % 2
            for j in range(4):
                pb, te, o0, n = pair[j // 2]
                tk = Q.add("tensor", lambda e, j=j, pb=pb, o0=o0, n=n: e.matmul(
                    PB[32 * j:32 * j + 17, 7, o0:512], V[:, g % 2, kt, 17 * j:17 * j + 17], P[:, pb, j % 2, 0:n],
                    start=kt == 0, stop=True, skip_group_check=True),
                    after=[pair[0][1], pair[1][1], loaded_v[g], o_free[0] if kt == 0 else None], mark="pv")
            for pb, *_ in pair:
                p_read[pb] = tk
            if kt < 4 * c + 3:
                return tk
            nchunk[0] += 1
            toc = o_free[0] = Q.add("scalar", lambda e: e.activation(osb[:, ob_], PB[:, 7, :], ACT.Copy),
                                    after=[tk, osb_free[ob_]], mark="oc")
            t1 = load(d16[:, ob_, :], osb[16:113:32, ob_, :].rearrange("p (a f) -> p a f", f=16), f"l_d{ob_}", [toc, d16_free[ob_]])

            def invert():
                t2 = d16_free[ob_] = Q.add("vector", lambda e: e.reciprocal(r16[:, ob_, :], d16[:, ob_, :]),
                                           after=[t1, r16_free[ob_]], mark="rd")
                t3 = r16_free[ob_] = Q.add("sync", lambda e: e.dma_start(
                    rd_d[ch].rearrange("j (a f) -> (j a) f", f=16), r16[:, ob_, :]), after=[t2], mark=f"w_rd{ob_}", dma=True)
                for j in range(4):
                    t4 = load(rden[32 * j:32 * j + 32, ob_, :], rd_d[ch, j].partition_broadcast(32), f"l_rd{ob_}", [t3, rd_free[ob_]])
                now["rd", ch] = t4

            def norm():
                need = [proj_tok[b - 1, 4 * c + i] for i in range(4)] if b > 0 else []
                ton = Q.add("gpsimd", lambda e: e.tensor_tensor(
                    ON[:, gi, 512 * c:512 * c + 512], osb[:, ob_], rden[:, ob_], ALU.mult), after=[now["rd", ch], toc, *need], mark="on")
                osb_free[ob_] = rd_free[ob_] = ton
                on_tok[b, gi, c] = ton
            late.append([4, invert])
            late.append([8, norm])
            return tk

        def group(g, pump):
            mu = list(max_units(g + 1)) if g < 15 else []
            done = [0]

            def unit(limit):
                if done[0] < min(limit, len(mu)):
                    mu[done[0]]()
                    done[0] += 1

            for i, (c, kt) in enumerate([(c, kt) for c in range(4) for kt in range(4 * c + 4)]):
                first = 11 if g == 0 else 0
                want = min(len(mu), -(-len(mu) * max(0, i + 1 - first) // (38 - first)))
                pbs = [(np_[0] + k) % NP for k in (0, 1)]
                np_[0] += 2
                st_one(g, 0, c, kt, 0, pbs[0])
                unit(want)
                p0 = st_one(g, 0, c, kt, 1, pbs[0])
                unit(want)
                if len(pend) == 2:
                    g_, *rest = pend.pop(0)
                    done_g[g_] = pv(g_, *rest)
                unit(want)
                st_one(g, 1, c, kt, 0, pbs[1])
                unit(want)
                p1 = st_one(g, 1, c, kt, 1, pbs[1])
                while done[0] < want:
                    unit(want)
                pend.append((g, c, kt, (p0, p1)))
                if i >= 2:
                    for x_ in pump:
                        x_[1] += x_[2]
                        while x_[1] >= 1:
                            x_[1] -= 1
                            next(x_[0], None)
                tick()
                if i == 9 and 0 < g and g + 2 < 16:
                    loaded[g + 2] = load_g(g + 2, [done_g[g - 1]])
                if i == 9 and g < 15:
                    loaded_v[g + 1] = load_v(g + 1, [done_g[g - 1]] if g > 0 else [])
                if g == 15 and 9 <= i < 9 + 3 * len(w_parts) and i % 3 == 0:
                    load_w13(w_parts[(i - 9) // 3])

        for g in (1, 2):
            loaded[g] = load_g(g, [])

        W13 = [nc.alloc_sbuf_tensor_at(f"W13{f}", [128, NE, 2 * I], F32, offset=at) for f, at in ((0, qo_at), (1, ko_at))]
        w_parts = ((0, 3), (3, 6), (6, 9), (9, 12), (12, 15), (15, NE))
        t_ew = {}
        assert NE * 2 * I * 4 <= 2 * 4 * T * 2

        def load_w13(part):
            lo, hi = part
            for f in (0, 1):
                t_ew["w13"] = load(W13[f][:, lo:hi], w13[f, :, lo:hi], "l_ew", [done_g[14]])

        ready = {}
        t_tail = {}
        hs_free = [None] * 3
        flat = {n: R[n][:, :, :].rearrange("p t e -> p (t e)") for n in ("sg", "rk", "sa")}
        hs = [flat["sg"][:, 0:256], flat["sg"][:, 256:512], flat["rk"][:, 0:256]]
        zr = flat["sa"][:, 0:256]
        hs_n = [0]

        def route(p):
            T0, PT = FIRST[p], TILES[p]
            sg, sb_, rk, cm, sa, selb = (R[n][:, 0:PT, :] for n in ("sg", "sb_", "rk", "cm", "sa", "selb"))
            gs, gt, gr, slot = sa[:, :, 0:4], sa[:, :, 4:8], sa[:, :, 8:12], sg
            wsum = R["wsum"][:, 0:PT]
            cnt, ntile, zidx, zpad = (R[n][:, :] for n in ("cnt", "ntile", "zidx", "zpad"))
            cend = R["cend"]
            n_i = NI[p] + 1
            tie, tic = (cm.rearrange("p t e -> p (t e)")[0:1, n_i * k:n_i * k + n_i] for k in (0, 1))
            k128, tix = fc_s[:, 0:PT], fc_s[0:1, MT:MT + n_i]
            o = MT + NI[0] + 1
            iotas, spare = fc_s[:, o:o + 1], fc_s[:, o + 1 + E * p:o + 1 + E * p + E]
            if p == 0:
                t_on = Q.add("gpsimd", lambda e: e.memset(R["onesb"][:, :], 1.0), mark="f_o")
                ready["ut"] = Q.add("gpsimd", lambda e: e.affine_select(
                    out=R["utri"][:, :], in_=R["onesb"][:, :], compare_op=ALU.is_gt, fill=0.0, base=0, pattern=[[1, 128]],
                    channel_multiplier=-1), after=[t_on], mark="f_u")
            while T0 + PT - 1 not in l_tok:
                yield
            last = [(l_tok[T0 + PT - 1], *([*ready["slots", p - 1], ready["z", p - 1], t_tail[p - 1]] if p else []))]

            def vec(fn, *more):
                last[0] = Q.add("vector", fn, after=[last[0], *more], mark="rt")

            def any_(fn, *more):
                last[0] = Q.add("gpsimd" if p == 0 else "vector", fn, after=[last[0], *more], mark="rg" if p == 0 else "rt")

            last[0] = Q.add("scalar", lambda e: e.activation(sg, L[:, T0:T0 + PT, :], ACT.Exp, scale=-1.0),
                            after=[last[0]], mark="sge")
            vec(lambda e: e.tensor_scalar(rk, sg, 1.0, None, ALU.add))
            yield
            vec(lambda e: e.reciprocal(sg, rk))
            yield
            any_(lambda e: e.tensor_tensor(sb_, sg, gbB[:, :].unsqueeze(1).broadcast_to([128, PT, 16]), ALU.add), t_rt)
            yield
            m4 = sb_.rearrange("p t (g m) -> p t g m", m=4)
            first = True
            for a in range(4):
                for c in range(a + 1, 4):
                    any_(lambda e, a=a, c=c, d=gs if first else gt: e.tensor_tensor(d, m4[:, :, :, a], m4[:, :, :, c], ALU.add))
                    yield
                    if not first:
                        vec(lambda e: e.tensor_tensor(gs, gs, gt, ALU.max))
                        yield
                    first = False
                    yield
            any_(lambda e: e.memset(gr, 0.0))
            yield
            any_(lambda e: e.memset(rk, 0.0))
            yield

            def ranks(vals, rank, tmp, n):
                for d in range(1, n):
                    lo, hi = vals[:, :, 0:n - d], vals[:, :, d:n]
                    vec(lambda e, lo=lo, hi=hi, d=d: e.tensor_tensor(tmp[:, :, 0:n - d], lo, hi, ALU.is_ge))
                    yield
                    any_(lambda e, d=d: e.tensor_tensor(rank[:, :, d:n], rank[:, :, d:n], tmp[:, :, 0:n - d], ALU.add))
                    yield
                    vec(lambda e, d=d: e.scalar_tensor_tensor(
                        out=rank[:, :, 0:n - d], in0=rank[:, :, 0:n - d], scalar=1.0, in1=tmp[:, :, 0:n - d],
                        op0=ALU.add, op1=ALU.subtract))
                    yield

            yield from ranks(gs, gr, gt, 4)
            vec(lambda e: e.tensor_scalar(gr, gr, 2.0, None, ALU.is_lt))
            yield
            vec(lambda e: e.tensor_scalar(gt, gr, -1.0, BIG, ALU.add, ALU.mult))
            yield
            any_(lambda e: e.tensor_tensor(m4, m4, gr.unsqueeze(3).broadcast_to([128, PT, 4, 4]), ALU.mult))
            yield
            any_(lambda e: e.tensor_tensor(m4, m4, gt.unsqueeze(3).broadcast_to([128, PT, 4, 4]), ALU.add))
            yield
            yield from ranks(sb_, rk, cm, 16)
            vec(lambda e: e.tensor_scalar(selb, rk, 4.0, None, ALU.is_lt))
            t_sel = last[0]
            yield
            vec(lambda e: e.tensor_tensor(cm, selb, sg, ALU.mult))
            yield
            vec(lambda e: e.tensor_reduce(wsum, cm, AX.X, ALU.add))
            yield
            vec(lambda e: e.tensor_scalar(wsum, wsum, 1e-20, None, ALU.add))
            yield
            vec(lambda e: e.reciprocal(wsum, wsum))
            yield
            any_(lambda e: e.tensor_tensor(cm, cm, wsum.unsqueeze(2).broadcast_to([128, PT, 16]), ALU.mult))
            yield
            vec(lambda e: e.tensor_scalar(cm, cm, 2.5, None, ALU.mult))
            yield
            for lo in range(0, PT, 32):
                n = min(32, PT - lo)
                for mat, dst in ((R["onesb"], sa), (R["utri"], slot)):
                    bank, free = unit_bank()
                    tk = Q.add("tensor", lambda e, lo=lo, n=n, mat=mat, bank=bank: e.matmul(
                        PB[:, bank, 0:16 * n], mat[:, :], selb[:, lo:lo + n, :].rearrange("p t e -> p (t e)"), start=True, stop=True),
                        after=[t_sel, ready["ut"], free], mark="s")
                    vec(lambda e, lo=lo, n=n, dst=dst, bank=bank: e.tensor_copy(
                        dst[:, lo:lo + n, :], PB[:, bank, 0:16 * n].rearrange("p (t e) -> p t e", e=16)), tk)
                    unit_done(last[0])
                    yield
            any_(lambda e: e.tensor_tensor(slot, slot, sa, ALU.subtract))
            yield
            bufs = [sa, sb_]
            d = 1
            while d < PT:
                a_, b_ = bufs
                vec(lambda e, a_=a_, b_=b_, d=d: e.tensor_copy(b_[:, 0:d, :], a_[:, 0:d, :]))
                yield
                any_(lambda e, a_=a_, b_=b_, d=d: e.tensor_tensor(b_[:, d:PT, :], a_[:, d:PT, :], a_[:, 0:PT - d, :], ALU.add))
                yield
                bufs = [b_, a_]
                d *= 2
                yield
            inc, other = bufs
            any_(lambda e: e.tensor_tensor(slot, slot, inc, ALU.add))
            yield
            vec(lambda e: e.tensor_copy(cnt, inc[:, PT - 1, :]))
            yield
            ticmp = other.rearrange("p t e -> p (t e)").rearrange("p (e t) -> p e t", e=16)
            vec(lambda e: e.tensor_tensor(ticmp, cnt.unsqueeze(2).broadcast_to([128, 16, PT]),
                                          k128.unsqueeze(1).broadcast_to([128, 16, PT]), ALU.is_gt), t_rt)
            yield
            vec(lambda e: e.tensor_reduce(ntile, ticmp, AX.X, ALU.add))
            yield
            vec(lambda e: e.tensor_copy(cend[:, 0, :], ntile))
            yield
            cur, d = 0, 1
            while d < 16:
                vec(lambda e, cur=cur, d=d: e.tensor_copy(cend[:, 1 - cur, 0:d], cend[:, cur, 0:d]))
                yield
                vec(lambda e, cur=cur, d=d: e.tensor_tensor(cend[:, 1 - cur, d:16], cend[:, cur, d:16], cend[:, cur, 0:16 - d], ALU.add))
                yield
                cur, d = 1 - cur, 2 * d
            ce_, base = cend[:, cur, :], cend[:, 1 - cur, :]
            vec(lambda e: e.tensor_tensor(base, ce_, ntile, ALU.subtract))
            yield
            vec(lambda e: e.tensor_scalar(base, base, 128.0, None, ALU.mult))
            yield
            vec(lambda e: e.tensor_tensor(slot, slot, base.unsqueeze(1).broadcast_to([128, PT, 16]), ALU.add))
            yield
            vec(lambda e: e.tensor_tensor(zidx, base, cnt, ALU.add))
            yield
            vec(lambda e: e.scalar_tensor_tensor(out=zidx, in0=zidx, scalar=iotas, in1=spare, op0=ALU.add, op1=ALU.subtract))
            yield
            vec(lambda e: e.scalar_tensor_tensor(out=zpad, in0=ntile, scalar=128.0, in1=cnt, op0=ALU.mult, op1=ALU.subtract))
            yield
            vec(lambda e: e.tensor_scalar(zpad, zpad, iotas, None, ALU.is_gt))
            yield
            vec(lambda e: e.tensor_tensor(zidx, zidx, zpad, ALU.mult))
            yield
            vec(lambda e: e.tensor_tensor(R["zidu"][:, p, :], zidx, spare, ALU.add))
            ready["zi", p] = last[0]
            yield
            sidx = other.rearrange("p t e -> p (t e)")[:, 0:4 * PT].rearrange("p (t j) -> p t j", j=4)
            for j in range(TOPK):
                for src, dst in ((slot, sidx[:, :, j]), (cm, wts[:, T0:T0 + PT, j])):
                    vec(lambda e, src=src, j=j: e.scalar_tensor_tensor(
                        out=inc, in0=rk, scalar=float(j), in1=src, op0=ALU.is_equal, op1=ALU.mult))
                    yield
                    vec(lambda e, dst=dst: e.tensor_reduce(dst, inc, AX.X, ALU.add))
                yield
            vec(lambda e: e.tensor_copy(sidu[:, T0:T0 + PT, :], sidx))
            ready["idx", p] = last[0]
            yield
            any_(lambda e: e.memset(tie, 0.0))
            yield
            for z in range(E):
                vec(lambda e, z=z: e.tensor_scalar(tic, tix, ce_[0:1, z:z + 1], None, ALU.is_ge))
                yield
                vec(lambda e: e.tensor_tensor(tie, tie, tic, ALU.add))
                yield
                if z % 3 == 2:
                    yield
            vec(lambda e: e.tensor_copy(tile_e[p][:, :], tie))
            ready["rt", p] = last[0]
            yield

        def scatter(p):
            ends = {}
            rows = {}
            t_z = Q.add("gpsimd", lambda e: e.memset(zr, 0.0), after=[ready["rt", p]], mark="f_z")
            for z in range(TILES[p] * TOPK, NI[p] + 1):
                t_tail[p] = Q.add("sync", lambda e, z=z: e.dma_start(xg_d[p][128 * z:128 * z + 128, :], zr),
                                  after=[t_z], mark=f"w_t{p}", dma=True)
            yield

            def fetch(t_):
                i, k = FIRST[p] + t_, (hs_n[0] + t_) % 3
                rows[t_] = load(hs[k], h2_d[128 * i:128 * i + 128, :], f"l_hs{k}", [h2_tok[i], hs_free[k], ready["rt", p]])

            fetch(0)
            fetch(1)
            for z in range(E):
                ready["z", p] = Q.add("gpsimd", lambda e, z=z: e.indirect_dma_start(
                    xg_d[p][:, :], bass.IndirectOffsetOnAxis(R["zidu"][:, p, z:z + 1], 0), zr, None),
                    after=[ready["zi", p], t_tail[p], t_z], mark=f"w_z{p}", dma=True)
                yield
            for t_ in range(TILES[p]):
                i, k = FIRST[p] + t_, (hs_n[0] + t_) % 3
                for j in range(TOPK):
                    ends[k] = hs_free[k] = Q.add("gpsimd", lambda e, i=i, j=j, k=k: e.indirect_dma_start(
                        xg_d[p][:, :], bass.IndirectOffsetOnAxis(sidu[:, i, j:j + 1], 0), hs[k], None),
                        after=[ready["idx", p], ready["z", p], rows[t_]], mark=f"w_s{p}{k}", dma=True)
                    yield
                if t_ + 2 < TILES[p]:
                    fetch(t_ + 2)
            hs_n[0] += TILES[p]
            ready["slots", p] = tuple(ends.values())

        def chain(*gens):
            for f in gens:
                yield from f

        def drain(f):
            for _ in f:
                pass

        part0 = chain(route(0), scatter(0))
        proj = [project(b) for b in range(4)]
        for g in range(16):
            pump = []
            if g % 4 == 0 and g > 0:
                pump.append([proj[g // 4 - 1], 0.0, 4])
            if g % 4 == 3:
                pump.append([proj[g // 4], -8.0, 2])
            if 8 <= g:
                pump.append([part0, 0.0, 0.7 if g == 12 else 1.7 if g > 12 else 1.4])
            group(g, pump)
            if g % 4 == 0 and g > 0:
                drain(pump[0][0])
        drain(part0)
        xq = nc.alloc_sbuf_tensor_at("xq", [128, 3, 256], F32, offset=ko_at + NE * 2 * I * 4)
        xT = nc.alloc_sbuf_tensor_at("xT", [128, 2, 2, 128], F32, offset=ko_at + NE * 2 * I * 4 + 3 * 256 * 4)
        assert NE * 2 * I * 4 + 5 * 256 * 4 <= 2 * 4 * T * 2
        rows0 = {m: load(xq[:, m], xg_d[0][128 * m:128 * m + 128, :], f"l_q{m}", [*ready["slots", 0], done_g[14]]) for m in range(3)}
        A.at = qo_at + NE * 2 * I * 4
        W2 = [A("W20", [128, NE, 256], F32)]
        GB = A("GB", [128, 4, 256], F32)
        assert A.at <= ko_at
        A.at = ko_at + NE * 2 * I * 4 + 5 * 256 * 4
        W2.append(A("W21", [128, NE, 256], F32))
        assert A.at <= v_at
        t_st = list(st_read)
        for lo, hi in ((0, 6), (6, 12), (12, NE)):
            for half, rows in ((0, 128), (1, 64)):
                t_ew["w2"] = Q.add("scalar", lambda e, half=half, rows=rows, lo=lo, hi=hi: e.dma_start(
                    W2[half][0:rows, lo:hi], w2[128 * half:128 * half + rows, lo:hi]), after=t_st, mark="l_ew2", dma=True)
        for x_ in pend:
            t_end = pv(*x_)

        A.at = v_at
        sl = A("sl", [128, 2, I], F32)
        ha = A("ha", [128, 2, I], F32)
        haT = A("haT", [128, 2, 2, 128], F32)
        yo = A("yo", [128, 2, 256], F32)
        XS = 6
        xs = A("xs", [128, XS, 256], F32)
        YG = 3
        yg = A("yg", [128, YG, 4, 256], F32)
        A.at = on_at
        acc = A("acc", [128, MT, 256], F32)
        assert A.at <= qo_at

        unit_banks[:] = [7]
        bank7[0] = o_free[0]
        xT_free = [done_g[14]] * 2
        xq_free = [done_g[14]] * 3
        xT_psum = [st_read[0], st_read[0]]
        gu_free = [st_read[1]] * 2
        sl_free = [t_end] * 2
        ha_free = [t_end] * 2
        ht_free = [tuple(unit_read[-3:])] * 2
        haT_free = [t_end] * 2
        y_free = [tuple(unit_read[-3:]), None]
        y_banks = [6]
        yo_free = [t_end] * 2
        xs_free = [t_end] * XS
        written = {}
        regs = {}

        def job_load(n, job):
            kind, p, i = job
            src, after = (xg_d[p], [ready["slots", p]]) if kind == "x" else (h2_d, [h2_tok[i]])
            if kind == "s":
                now["xs", i] = load(xs[:, n % XS], x1_d[128 * i:128 * i + 128, :], f"l_x1{n % XS}", [x1_tok[i], xs_free[n % XS]])
            return load(xq[:, n % 3], src[128 * i:128 * i + 128, :], f"l_q{n % 3}", [*after, xq_free[n % 3]])

        def job_in(n, job, tl):
            k = n % 2
            for f in (0, 1):
                t = Q.add("tensor", lambda e, f=f: e.transpose(PB[:, k, 128 * f:128 * f + 128], xq[:, n % 3, 128 * f:128 * f + 128], ident[:, :]),
                          after=[tl, xT_psum[k]], mark="jt")
            xq_free[n % 3] = t
            t = Q.add("scalar", lambda e: e.activation(xT[:, k], PB[:, k, 0:256].rearrange("p (f q) -> p f q", f=2), ACT.Copy),
                      after=[t, xT_free[k]], mark="xT")
            xT_psum[k] = t
            return t

        RB = 8

        def expert_of(job, eng):
            kind, p, i = job
            if kind != "x":
                return None
            if (p, i) not in regs:
                n = min(RB, NI[p] + 1 - i)
                half = i // RB % 2 * RB
                eng.load(pe_regs[half:half + n], tile_e[p][0:1, i:i + n])
                for j in range(n):
                    regs[p, i + j] = eng.snap(pe_regs[half + j], min_val=0, max_val=E)
            return regs[p, i]

        pe_regs = []

        def job_gate(n, job, tx):
            kind, p, i = job
            k = n % 2
            need = [ready["rt", p], t_ew["w13"]]
            for f in (0, 1):
                def mm(e, f=f):
                    ex = expert_of(job, e)
                    w = W13[f][:, E, :] if ex is None else W13[f][:, bass.ds(ex, 1), :]
                    return e.matmul(PB[:, 2 + k, 0:2 * I], xT[:, k, f, :], w, start=f == 0, stop=f == 1)
                t = Q.add("tensor", mm, after=[tx, gu_free[k], *need], mark="gu")
            xT_free[k] = t
            ts = Q.add("scalar", lambda e: e.activation(sl[:, k], PB[:, 2 + k, 0:I], ACT.Silu), after=[t, sl_free[k]], mark="sl")
            t = Q.add("vector", lambda e: e.tensor_tensor(ha[:, k], sl[:, k], PB[:, 2 + k, I:2 * I], ALU.mult),
                      after=[ts, ha_free[k]], mark="ha")
            gu_free[k] = sl_free[k] = t
            return t

        def job_turn(n, job, th):
            k = n % 2
            Q.add("tensor", lambda e: e.transpose(PB[:, 4 + k, 0:128], ha[:, k, 0:128], ident[:, :]), after=[th, ht_free[k]], mark="ht")
            t = Q.add("tensor", lambda e: e.transpose(PB[0:64, 4 + k, 128:256], ha[:, k, 128:192], ident[:, :]), mark="ht")
            ha_free[k] = t
            Q.add("scalar", lambda e: e.activation(haT[:, k, 0, :], PB[:, 4 + k, 0:128], ACT.Copy), after=[t, haT_free[k]], mark="haT")
            t = Q.add("scalar", lambda e: e.activation(haT[0:64, k, 1, :], PB[0:64, 4 + k, 128:256], ACT.Copy), mark="haT")
            ht_free[k] = t
            return t

        def job_down(n, job, ta, tl):
            kind, p, i = job
            k, w = n % 2, n % len(y_banks)
            bank = y_banks[w]

            def mm(e, half):
                ex = expert_of(job, e)
                rows = slice(0, 128) if half == 0 else slice(0, 64)
                w = W2[half][rows, E, :] if ex is None else W2[half][rows, bass.ds(ex, 1), :]
                return e.matmul(PB[:, bank, 0:256], haT[rows, k, half, :], w, start=half == 0, stop=half == 1)
            Q.add("tensor", lambda e: mm(e, 0), after=[ta, y_free[w], t_ew["w2"]], mark="dn")
            t = Q.add("tensor", lambda e: mm(e, 1), mark="dn")
            haT_free[k] = t
            if kind == "x":
                t = Q.add("vector", lambda e: e.tensor_copy(yo[:, k], PB[:, bank, 0:256]), after=[t, yo_free[k]], mark="yo")
                y_free[w] = t
                yo_free[k] = Q.add("sync", lambda e: e.dma_start(y_d[p][128 * i:128 * i + 128, :], yo[:, k]), after=[t],
                                   mark=f"w_y{p}{k}", dma=True)
                written["y", p, k] = yo_free[k]
            else:
                t = Q.add("vector", lambda e: e.tensor_tensor(yo[:, k], PB[:, bank, 0:256], acc[:, i - FIRST[p], :], ALU.add),
                          after=[t, yo_free[k], now["acc", i]], mark="yo")
                y_free[w] = now["used", i] = t
                t = Q.add("vector", lambda e: e.tensor_tensor(yo[:, k], yo[:, k], GB[:, i // 16], ALU.mult), after=[t, t_gb], mark="fin")
                t = Q.add("vector", lambda e: e.tensor_tensor(yo[:, k], yo[:, k], xs[:, n % XS], ALU.add),
                          after=[t, now["xs", i]], mark="fin")
                xs_free[n % XS] = t
                yo_free[k] = Q.add("sync", lambda e: e.dma_start(out[128 * i:128 * i + 128, :], yo[:, k]), after=[t],
                                   mark=f"w_o{k}", dma=True)

        yg_free = [t_end] * YG

        def collect(p):
            wy = [written["y", p, k] for k in (0, 1)]
            if p == 0:
                wy += [proj_tok[3, t_] for t_ in range(16)]
            rows = {}

            def fetch(t_):
                i, k = FIRST[p] + t_, t_ % YG
                for j in range(TOPK):
                    rows[t_] = Q.add("gpsimd", lambda e, j=j: e.indirect_dma_start(
                        yg[:, k, j, :], None, y_d[p][:, :], bass.IndirectOffsetOnAxis(sidu[:, i, j:j + 1], 0)),
                        after=[*wy, ready["idx", p], yg_free[k]], mark=f"l_yg{k}", dma=True)

            fetch(0)
            fetch(1)
            for t_ in range(TILES[p]):
                i, k = FIRST[p] + t_, t_ % YG
                if t_ + 2 < TILES[p]:
                    fetch(t_ + 2)
                yield
                used = None
                if p > 0:
                    while ("used", t_) not in now:
                        yield
                    used = now["used", t_]
                t = Q.add("vector", lambda e, t_=t_, i=i, k=k: e.tensor_scalar(
                    acc[:, t_, :], yg[:, k, 0, :], wts[:, i, 0:1], None, ALU.mult), after=[rows[t_], used, ready["idx", p]], mark="cb")
                for j in range(1, TOPK):
                    yield
                    t = Q.add("vector", lambda e, t_=t_, i=i, k=k, j=j: e.scalar_tensor_tensor(
                        out=acc[:, t_, :], in0=yg[:, k, j, :], scalar=wts[:, i, j:j + 1], in1=acc[:, t_, :], op0=ALU.mult, op1=ALU.add),
                        after=[t], mark="cb")
                yg_free[k] = now["acc", i] = t

        lag = []
        count = [0]

        def run(jobs, *pumps, rows=None):
            pumps = [[f, 0.0, rate] for f, rate in pumps]
            n0 = count[0]
            rows = rows or {}

            def ahead(m):
                if m < len(jobs) and m not in rows:
                    rows[m] = job_load(n0 + m, jobs[m])

            ahead(0)
            ahead(1)
            for m, job in enumerate([*jobs, None, None, None]):
                if job is not None:
                    n = count[0]
                    count[0] += 1
                    lag.append([n, job, 0, None, rows.get(m)])
                for x_ in list(lag):
                    n, jb, st_, tk, tl = x_
                    if st_ == 0:
                        x_[3] = job_in(n, jb, tl)
                        ahead(m + 2)
                    elif st_ == 1:
                        x_[3] = job_gate(n, jb, tk)
                    elif st_ == 2:
                        x_[3] = job_turn(n, jb, tk)
                    else:
                        job_down(n, jb, tk, tl)
                        lag.remove(x_)
                    x_[2] += 1
                for f in pumps:
                    f[1] += f[2]
                    while f[1] >= 1:
                        f[1] -= 1
                        next(f[0], None)
            for f in pumps:
                drain(f[0])

        routed = [[("x", p, i) for i in range(NI[p])] for p in range(PARTS)]
        while late:
            tick()
        run(routed[0], (chain(proj[3], route(1), scatter(1)), 2.65), rows=rows0)
        t_gb = load(GB[:, :, :], mod_d[1].partition_broadcast(128), "l_gb", [t_end])
        y_banks.append(7)
        y_free[:] = [(y_free[0], unit_read[-1])] * 2
        run(routed[1], (collect(0), 1))
        run([("s", p, FIRST[p] + i) for p in range(PARTS) for i in range(TILES[p])], (collect(1), 2.3))
        Q.pause("sync", [(k, v) for k, v in Q.everything() if k.startswith("w_")])

        block = ctx.enter_context(nc.Block())

        @block.sync
        def _(eng):
            Q.play("sync", eng)

        @block.tensor
        def _(eng):
            pe_regs.extend(eng.alloc_register(f"expert{j}") for j in range(2 * RB))
            Q.play("tensor", eng)

        @block.vector
        def _(eng):
            Q.play("vector", eng)

        @block.scalar
        def _(eng):
            Q.play("scalar", eng)

        @block.gpsimd
        def _(eng):
            Q.play("gpsimd", eng)


def tables():
    inv = (1.0 / (np.float32(10000.0) ** (np.arange(0, HD, 2, dtype=np.float32) / np.float32(HD)))).astype(np.float32)
    fr = np.arange(T, dtype=np.float32)[:, None] * inv[None, :]
    rope = np.concatenate([np.sin(fr.astype(np.float64)), np.cos(fr.astype(np.float64))], -1).astype(np.float32)
    s, c = rope[:, 0::2].T, rope[:, 1::2].T
    k = np.arange(128)
    cons = np.zeros((128, 2, 128), np.float32)
    cons[:, 0, :] = np.eye(128, dtype=np.float32)
    cons[:, 1, :] = np.where(k[None, :] > k[:, None], np.float32(-BIG), np.float32(0))
    n = NI[0] + 1
    fcon = np.zeros((128, MT + n + 1 + 2 * E), np.float32)
    fcon[:, 0:MT] = 128 * np.arange(MT)
    fcon[:, MT:MT + n] = np.arange(n)
    fcon[:, MT + n] = k
    for p in range(PARTS):
        fcon[:, MT + 1 + n + E * p:MT + 1 + n + E * p + E] = (NI[p] + 1 + np.arange(E)[None, :]) * 128 + k[:, None]
    return np.ascontiguousarray(np.tile(c, (16, 1))), np.ascontiguousarray(np.tile(s, (16, 1))), cons, fcon


def kernel(L0_attn_x, L0_attn_qkv_w, L0_attn_qkv_b, L0_attn_out_w, L0_attn_out_b, L0_ffn_gate_w, L0_ffn_gate_bias,
           L0_ffn_w1, L0_ffn_w2, L0_ffn_w3, L0_ffn_ws1, L0_ffn_ws2, L0_ffn_ws3, L0_c, L0_wmod):
    import concourse.bacc as bacc
    from concourse.bass_utils import run_bass_kernel_spmd

    a = np.ascontiguousarray
    qkv_w, qkv_b = np.asarray(L0_attn_qkv_w), np.asarray(L0_attn_qkv_b)
    head = np.arange(H)[:, None] * HD
    cols = [(z * D + head + 2 * np.arange(8)[None, :] + o).reshape(-1) for z in (0, 1) for o in (0, 1)]
    wo = np.zeros((4, 4, 32, D), np.float32)
    wo[:, :, 0:HD, :] = np.asarray(L0_attn_out_w).reshape(4, 4, HD, D)
    bv = np.zeros((4, 4, 32), np.float32)
    bv[:, :, 0:HD] = qkv_b[2 * D:].reshape(4, 4, HD)
    w1 = np.concatenate([np.asarray(L0_ffn_w1), np.asarray(L0_ffn_ws1)[None]], 0)
    w3 = np.concatenate([np.asarray(L0_ffn_w3), np.asarray(L0_ffn_ws3)[None]], 0)
    w2 = np.concatenate([np.asarray(L0_ffn_w2), np.asarray(L0_ffn_ws2)[None]], 0)
    w13 = np.concatenate([w1, w3], 1).transpose(2, 0, 1).reshape(2, 128, NE, 2 * I)
    ropec, ropes, cons, fcon = tables()
    arrays = {
        "x": a(np.asarray(L0_attn_x).reshape(N, D)),
        "wqk": a(qkv_w[:, np.concatenate(cols)]),
        "wv": a(qkv_w[:, 2 * D:]),
        "bqk": a(np.stack([qkv_b[c] for c in cols], 1)),
        "bv": a(bv.reshape(4, 128).T),
        "wo": a(wo.reshape(4, 128, D).transpose(1, 0, 2)),
        "ob": a(np.asarray(L0_attn_out_b)),
        "gw": a(np.asarray(L0_ffn_gate_w).T),
        "gbias": a(np.asarray(L0_ffn_gate_bias)),
        "w13": a(w13),
        "w2": a(w2.transpose(2, 0, 1)),
        "cT": a(np.asarray(L0_c).T.reshape(2, 128, B).transpose(1, 0, 2)),
        "wmod": a(np.asarray(L0_wmod)),
        "ropec": ropec,
        "ropes": ropes,
        "consts": cons,
        "fconst": fcon,
    }
    nc = bacc.Bacc("TRN2", target_bir_lowering=False, num_devices=1)
    args = {n: nc.dram_tensor(f"in_{n}", v.shape, mybir.dt.from_np(v.dtype), kind="ExternalInput").ap()
            for n, v in arrays.items()}
    args["out"] = nc.dram_tensor("out_0", (N, D), F32, kind="ExternalOutput").ap()
    program(nc, **args)
    got = run_bass_kernel_spmd(nc, [{f"in_{n}": v for n, v in arrays.items()}], core_ids=[0])
    return got.results[0]["out_0"].reshape(B, T, D)
```
